# Optimizing a Trainium2 kernel written in Bass

```python
import numpy as np
import jax
import jax.numpy as jnp

def _softmax(x, axis=-1):
    return jax.nn.softmax(x, axis=axis)

def _gelu(x):
    return jax.nn.gelu(x, approximate=True)

def _silu(x):
    return jax.nn.silu(x)

def _sigmoid(x):
    return jax.nn.sigmoid(x)

def _layernorm(x, axis=-1, eps=1e-05):
    m = jnp.mean(x, axis=axis, keepdims=True)
    v = jnp.var(x, axis=axis, keepdims=True)
    return (x - m) / jnp.sqrt(v + eps)

def _scatter_add(tgt, idx, src, axis=0):
    return tgt.at[idx].add(src)

def _segment_sum(src, seg, n):
    return jax.ops.segment_sum(src, seg, n)
kernel_name = 'mk_adaln_d1_jaxref_r8_e95892'

def setup_inputs(seed: int=0):
    np.random.seed(seed)
    _w = jnp.asarray

    def _L0_attn_setup():
        import math
        import jax, jax.numpy as jnp
        import numpy as np
        L, D, H, F = (4, 128, 16, 512)
        HD = D // H
        EPS = 1e-05

        def get_alibi_slopes(num_heads):
            closest = 2 ** math.floor(math.log2(num_heads))
            base = 2 ** (-2 ** (-(math.log2(closest) - 3)))
            slopes = base ** np.arange(1, closest + 1)
            if closest != num_heads:
                extra_base = 2 ** (-2 ** (-(math.log2(2 * closest) - 3)))
                extra = extra_base ** np.arange(1, 2 * (num_heads - closest) + 1, 2)
                slopes = np.concatenate([slopes, extra])
            return jnp.asarray(slopes, dtype=jnp.float32)

        def build_mask(num_heads, T):
            pos = jnp.arange(T)
            dist = pos[None, :] - pos[:, None]
            alibi = get_alibi_slopes(num_heads)[:, None, None] * dist[None]
            causal = jnp.where(dist > 0, -jnp.inf, 0.0).astype(jnp.float32)
            return causal[None] + alibi

        def layer_norm(x, w, b):
            mu = jnp.mean(x, axis=-1, keepdims=True)
            var = jnp.mean(jnp.square(x - mu), axis=-1, keepdims=True)
            return (x - mu) * jax.lax.rsqrt(var + EPS) * w + b

        def mha(x, mask, Wi, bi, Wo, bo):
            B, T, _ = x.shape
            qkv = x @ Wi.T + bi
            q, k, v = jnp.split(qkv, 3, axis=-1)
            q = q.reshape(B, T, H, HD).transpose(0, 2, 1, 3)
            k = k.reshape(B, T, H, HD).transpose(0, 2, 1, 3)
            v = v.reshape(B, T, H, HD).transpose(0, 2, 1, 3)
            scores = jnp.einsum('bhqd,bhkd->bhqk', q, k) / math.sqrt(HD)
            scores = scores + mask[None]
            attn = jax.nn.softmax(scores, axis=-1)
            out = jnp.einsum('bhqk,bhkd->bhqd', attn, v)
            out = out.transpose(0, 2, 1, 3).reshape(B, T, D)
            return out @ Wo.T + bo
        key = jax.random.key(seed)
        ks = jax.random.split(key, 13)
        s = 0.02
        inp = {'x': jax.random.normal(ks[0], (2, 256, D), dtype=jnp.float32), 'in_proj_w': jax.random.normal(ks[1], (L, 3 * D, D), dtype=jnp.float32) * s, 'in_proj_b': jnp.zeros((L, 3 * D), dtype=jnp.float32), 'out_proj_w': jax.random.normal(ks[2], (L, D, D), dtype=jnp.float32) * s, 'out_proj_b': jnp.zeros((L, D), dtype=jnp.float32), 'ffn1_w': jax.random.normal(ks[3], (L, F, D), dtype=jnp.float32) * s, 'ffn1_b': jnp.zeros((L, F), dtype=jnp.float32), 'ffn2_w': jax.random.normal(ks[4], (L, D, F), dtype=jnp.float32) * s, 'ffn2_b': jnp.zeros((L, D), dtype=jnp.float32), 'ln1_w': jnp.ones((L, D), dtype=jnp.float32), 'ln1_b': jnp.zeros((L, D), dtype=jnp.float32), 'ln2_w': jnp.ones((L, D), dtype=jnp.float32), 'ln2_b': jnp.zeros((L, D), dtype=jnp.float32), 'final_w': jnp.ones((D,), dtype=jnp.float32), 'final_b': jnp.zeros((D,), dtype=jnp.float32)}
        return inp
    _L0_attn_in = _L0_attn_setup()

    def _L0_ffn_setup():
        import jax, jax.numpy as jnp
        import numpy as np
        B, T, D, H, E = (4, 256, 128, 256, 8)
        TOP_K = int(E * 0.25)
        key = jax.random.key(seed)
        ks = jax.random.split(key, 6)
        x = jax.random.normal(ks[0], (B, T, D), dtype=jnp.float32)
        gate = jax.random.normal(ks[1], (D, E), dtype=jnp.float32)
        W1 = jax.random.normal(ks[2], (E, D, H), dtype=jnp.float32) * D ** (-0.5)
        b1 = jnp.zeros((E, H), dtype=jnp.float32)
        W2 = jax.random.normal(ks[3], (E, H, D), dtype=jnp.float32) * H ** (-0.5)
        b2 = jnp.zeros((E, D), dtype=jnp.float32)
        return {'x': x, 'gate': gate, 'W1': W1, 'b1': b1, 'W2': W2, 'b2': b2}
    _L0_ffn_in = _L0_ffn_setup()
    _L0_c = _w((lambda *s: np.random.randn(*s).astype(np.float32) * 0.05)(16, 128))
    _L0_wmod = _w((lambda *s: np.random.randn(*s).astype(np.float32) * 0.05)(128, 6 * 128) * 128 ** (-0.5))
    _d = {'L0_attn_x': _L0_attn_in['x'], 'L0_attn_in_proj_w': _L0_attn_in['in_proj_w'], 'L0_attn_in_proj_b': _L0_attn_in['in_proj_b'], 'L0_attn_out_proj_w': _L0_attn_in['out_proj_w'], 'L0_attn_out_proj_b': _L0_attn_in['out_proj_b'], 'L0_attn_ffn1_w': _L0_attn_in['ffn1_w'], 'L0_attn_ffn1_b': _L0_attn_in['ffn1_b'], 'L0_attn_ffn2_w': _L0_attn_in['ffn2_w'], 'L0_attn_ffn2_b': _L0_attn_in['ffn2_b'], 'L0_attn_ln1_w': _L0_attn_in['ln1_w'], 'L0_attn_ln1_b': _L0_attn_in['ln1_b'], 'L0_attn_ln2_w': _L0_attn_in['ln2_w'], 'L0_attn_ln2_b': _L0_attn_in['ln2_b'], 'L0_attn_final_w': _L0_attn_in['final_w'], 'L0_attn_final_b': _L0_attn_in['final_b'], 'L0_ffn_gate': _L0_ffn_in['gate'], 'L0_ffn_W1': _L0_ffn_in['W1'], 'L0_ffn_b1': _L0_ffn_in['b1'], 'L0_ffn_W2': _L0_ffn_in['W2'], 'L0_ffn_b2': _L0_ffn_in['b2'], 'L0_c': _L0_c, 'L0_wmod': _L0_wmod}
    _x0 = _d['L0_attn_x']
    _d['L0_attn_x'] = jax.random.normal(jax.random.fold_in(jax.random.key(seed), 1), (16, 512, 128), dtype=_x0.dtype)
    del _x0
    return _d

def reference(L0_attn_x, L0_attn_in_proj_w, L0_attn_in_proj_b, L0_attn_out_proj_w, L0_attn_out_proj_b, L0_attn_ffn1_w, L0_attn_ffn1_b, L0_attn_ffn2_w, L0_attn_ffn2_b, L0_attn_ln1_w, L0_attn_ln1_b, L0_attn_ln2_w, L0_attn_ln2_b, L0_attn_final_w, L0_attn_final_b, L0_ffn_gate, L0_ffn_W1, L0_ffn_b1, L0_ffn_W2, L0_ffn_b2, L0_c, L0_wmod):

    def _L0_attn_ref(x, in_proj_w, in_proj_b, out_proj_w, out_proj_b, ffn1_w, ffn1_b, ffn2_w, ffn2_b, ln1_w, ln1_b, ln2_w, ln2_b, final_w, final_b):
        import math
        import jax, jax.numpy as jnp
        import numpy as np
        L, D, H, F = (4, 128, 16, 512)
        HD = D // H
        EPS = 1e-05

        def get_alibi_slopes(num_heads):
            closest = 2 ** math.floor(math.log2(num_heads))
            base = 2 ** (-2 ** (-(math.log2(closest) - 3)))
            slopes = base ** np.arange(1, closest + 1)
            if closest != num_heads:
                extra_base = 2 ** (-2 ** (-(math.log2(2 * closest) - 3)))
                extra = extra_base ** np.arange(1, 2 * (num_heads - closest) + 1, 2)
                slopes = np.concatenate([slopes, extra])
            return jnp.asarray(slopes, dtype=jnp.float32)

        def build_mask(num_heads, T):
            pos = jnp.arange(T)
            dist = pos[None, :] - pos[:, None]
            alibi = get_alibi_slopes(num_heads)[:, None, None] * dist[None]
            causal = jnp.where(dist > 0, -jnp.inf, 0.0).astype(jnp.float32)
            return causal[None] + alibi

        def layer_norm(x, w, b):
            mu = jnp.mean(x, axis=-1, keepdims=True)
            var = jnp.mean(jnp.square(x - mu), axis=-1, keepdims=True)
            return (x - mu) * jax.lax.rsqrt(var + EPS) * w + b

        def mha(x, mask, Wi, bi, Wo, bo):
            B, T, _ = x.shape
            qkv = x @ Wi.T + bi
            q, k, v = jnp.split(qkv, 3, axis=-1)
            q = q.reshape(B, T, H, HD).transpose(0, 2, 1, 3)
            k = k.reshape(B, T, H, HD).transpose(0, 2, 1, 3)
            v = v.reshape(B, T, H, HD).transpose(0, 2, 1, 3)
            scores = jnp.einsum('bhqd,bhkd->bhqk', q, k) / math.sqrt(HD)
            scores = scores + mask[None]
            attn = jax.nn.softmax(scores, axis=-1)
            out = jnp.einsum('bhqk,bhkd->bhqd', attn, v)
            out = out.transpose(0, 2, 1, 3).reshape(B, T, D)
            return out @ Wo.T + bo
        T = x.shape[1]
        mask = build_mask(H, T)
        for i in range(L):
            xn = layer_norm(x, ln1_w[i], ln1_b[i])
            x = x + mha(xn, mask, in_proj_w[i], in_proj_b[i], out_proj_w[i], out_proj_b[i])
            xn = layer_norm(x, ln2_w[i], ln2_b[i])
            h = jax.nn.gelu(xn @ ffn1_w[i].T + ffn1_b[i], approximate=False)
            x = x + (h @ ffn2_w[i].T + ffn2_b[i])
        return layer_norm(x, final_w, final_b)

    def _L0_ffn_ref(x, gate, W1, b1, W2, b2):
        import jax, jax.numpy as jnp
        import numpy as np
        B, T, D, H, E = (4, 256, 128, 256, 8)
        TOP_K = int(E * 0.25)
        raw_gate = jax.nn.softmax(jnp.einsum('btd,de->bte', x, gate), axis=-1)
        topk_scores, topk_idx = jax.lax.top_k(raw_gate, TOP_K)
        mask = jax.nn.one_hot(topk_idx, E, dtype=raw_gate.dtype).sum(axis=-2)
        gate_topk = mask * raw_gate
        gate_topk = gate_topk / jnp.maximum(gate_topk.sum(axis=-1, keepdims=True), 1e-12)
        h = jax.nn.relu(jnp.einsum('btd,edh->beth', x, W1) + b1[None, :, None, :])
        expert_out = jnp.einsum('beth,ehd->betd', h, W2) + b2[None, :, None, :]
        out = jnp.einsum('bte,betd->btd', gate_topk, expert_out)
        return out
    x = L0_attn_x
    mod = (_silu(L0_c) @ L0_wmod).reshape(L0_c.shape[0], 6, 1, -1)
    sa, ca, ga, sb, cb, gb = (mod[:, 0], mod[:, 1], mod[:, 2], mod[:, 3], mod[:, 4], mod[:, 5])
    ga = (2 * (ga >= 0) - 1) * jnp.maximum(jnp.abs(ga), 0.25)
    gb = (2 * (gb >= 0) - 1) * jnp.maximum(jnp.abs(gb), 0.25)
    h = _layernorm(x, axis=-1) * (1 + ca) + sa
    x = x + ga * _L0_attn_ref(h, L0_attn_in_proj_w, L0_attn_in_proj_b, L0_attn_out_proj_w, L0_attn_out_proj_b, L0_attn_ffn1_w, L0_attn_ffn1_b, L0_attn_ffn2_w, L0_attn_ffn2_b, L0_attn_ln1_w, L0_attn_ln1_b, L0_attn_ln2_w, L0_attn_ln2_b, L0_attn_final_w, L0_attn_final_b)
    h = _layernorm(x, axis=-1) * (1 + cb) + sb
    x = x + gb * _L0_ffn_ref(h, L0_ffn_gate, L0_ffn_W1, L0_ffn_b1, L0_ffn_W2, L0_ffn_b2)
    return x

_drawn_inputs = setup_inputs


def setup_inputs(seed=0):
    import zlib

    import numpy as np

    out = dict(_drawn_inputs(seed))
    spreads = {'L0_attn_in_proj_b': (0.0, 0.614),
     'L0_attn_out_proj_b': (0.0, 0.345),
     'L0_attn_ffn1_b': (0.0, 0.564),
     'L0_attn_ffn2_b': (0.0, 0.355),
     'L0_attn_ln1_w': (1.0, 0.6),
     'L0_attn_ln1_b': (0.0, 0.8),
     'L0_attn_ln2_w': (1.0, 0.6),
     'L0_attn_ln2_b': (0.0, 2.0),
     'L0_attn_final_w': (1.0, 0.2),
     'L0_attn_final_b': (0.0, 0.315),
     'L0_ffn_b1': (0.0, 0.512),
     'L0_ffn_b2': (0.0, 0.36)}
    factors = {'L0_attn_in_proj_w': 5.683, 'L0_attn_out_proj_w': 3.536}
    for name, (base, spread) in spreads.items():
        noise = np.random.default_rng([zlib.crc32(name.encode()), seed]).standard_normal(out[name].shape)
        drawn = base * np.exp(spread * noise) if base else spread * noise
        out[name] = jnp.asarray(drawn.astype(out[name].dtype))
    for name, factor in factors.items():
        out[name] = (out[name] * factor).astype(out[name].dtype)
    return out
```

```python
import concourse.bass as bass
from concourse import mybir
from contextlib import ExitStack
import math
import numpy as np

F32 = mybir.dt.float32
BF16 = mybir.dt.bfloat16
ALU = mybir.AluOpType
ACT = mybir.ActivationFunctionType
AX = mybir.AxisListType

P = 128
D = 128
H, HD = 16, 8
QUADS = H // 4
KROW = 96
M_ROW = 6 * HD
ALIBI_ROW = M_ROW + 2
STEP_ROW = KROW
GROUP_ROW = STEP_ROW + 15
KSTEP = GROUP_ROW
EPS = 1e-5
VOCT = 32
E = 8
EH = 2

SCORE_TILES = [(0, (0, 1, 2, 3)), (1, (0, 1)), (1, (2, 3))] + [(i, (a,)) for i in (2, 3) for a in range(4)]
NSCORE = len(SCORE_TILES) * QUADS
MISC = {2: [("ln1T", 2)], 3: [("oT0", -1), ("oT1", -1)], 4: [("q", 2)], 5: [("onT", -1), ("k", 2)], 6: [("v", 1)],
        7: [("proj", -1)], 10: [("ln2T", -1)], 11: [("ffn1_0", -1), ("ffn1_1", -1), ("ffn1_2", -1), ("ffn1_3", -1)],
        12: [("ffn2_0", -1)], 13: [("ffn2_1", -1)], 14: [("mT", 1)]}


def score_slots():
    out = [[] for _ in range(16)]
    for t in range(NSCORE):
        out[t * 13 // NSCORE].append(t)
    return out


SCORES = score_slots()


def work_tiles():
    out = []
    for s in range(16):
        out += [("score", 1, t) for t in SCORES[s]] + [(name, off, None) for name, off in MISC.get(s, [])]
    assert len(out) % 2 == 0
    return out


WORK = work_tiles()
WQK = 2 * D + 4
WV = 2 * D
WOF = 2 * D + 4 * D + 4 * D + D + 6


def transformer_program(nc, NB, L, T, io):
    TB = T // P
    NSTEP = NB * L
    xs, wqk_d, wv_d, wof_d, qc_d, kc_d, id_d, idb_d = (io[k] for k in ("xs", "wqk", "wv", "wof", "qc", "kc", "ident", "identb"))
    scr = [io["scr0"], io["scr1"]]
    with ExitStack() as ctx:
        def sb(name, shape, dt=F32):
            return ctx.enter_context(nc.sbuf_tensor(name, shape, dt))

        def two(name, shape, dt=F32):
            return [sb(f"{name}{i}", shape, dt) for i in range(2)]

        def sem(name):
            return ctx.enter_context(nc.semaphore(name))

        def sems(name, n=2):
            return [sem(f"{name}{i}") for i in range(n)]

        x_ln = two("x_ln", [P, TB, D])
        x_res = two("x_res", [P, TB, D])
        wqk = two("w_qk", [P, WQK])
        wv = two("w_v", [P, WV])
        wof = two("w_of", [P, WOF])
        QS = two("q_stack", [P, H, T], BF16)
        KS = two("k_stack", [P, H, T], BF16)
        Vp = two("v_padded", [P, TB, H, VOCT])
        xnT = two("xnT", [P, T])
        PT = sb("probsT", [P, 4, 4, T])
        st1 = sb("st1", [P, TB, 6])
        mv1 = sb("mv1", [P, TB, 2])
        rs1 = sb("rs1", [P, TB])
        xh1 = sb("xh1", [P, TB, D])
        st2 = sb("st2", [P, TB, 6])
        mv2 = sb("mv2", [P, TB, 2])
        rs2 = sb("rs2", [P, TB])
        xh2 = sb("xh2", [P, TB, D])
        nhalf = sb("nhalf", [P, TB])
        bqk_s = sb("bqk_s", [P, 1])
        qscale = sb("qscale", [P, 1])
        word = sb("words", [1, 17])
        qk32 = sb("qk32", [P, 2, T])
        qk_r = sb("qk_rest", [P, 2, T])
        parts = sb("parts", [P, 2, 3, T], BF16)
        zero2 = sb("zero2", [2, H * T // 2], BF16)
        nmax = sb("nmax", [P, H, TB])
        nm_p = sb("nm_parts", [P, 2, H, TB], BF16)
        nm_r = sb("nm_rest", [P, H, TB])
        nmT = sb("nmT", [P, P], BF16)
        oraw = sb("oraw", [P, 2, T])
        rsum = sb("rsum", [P, TB, H])
        on = sb("on", [P, TB, H, HD])
        onT = sb("onT", [P, T])
        xb = sb("xb", [P, TB, D])
        x1 = sb("x1", [P, TB, D])
        x1b = sb("x1b", [P, TB, D])
        xnT2 = sb("xnT2", [P, T])
        hT = sb("hT", [P, 4, T])
        xo = two("xo", [P, TB, D])
        ident = sb("ident", [P, P])
        identb = sb("identb", [P, P], BF16)

        ST = [ctx.enter_context(nc.psum_tensor(f"scoresT{i}", [P, 2, T], F32)) for i in range(2)]
        PV = [ctx.enter_context(nc.psum_tensor(f"pv{i}", [P, T], F32)) for i in range(2)]
        W = [ctx.enter_context(nc.psum_tensor(f"work{i}", [P, T], F32)) for i in range(2)]

        const_in = sem("const_in")
        x_ln_in, x_res_in, wqk_in, wv_in, wof_in = (sems(n) for n in ("x_ln_in", "x_res_in", "wqk_in", "wv_in", "wof_in"))
        parts_out = sems("parts_out")
        stack_in = [sems("stack_in_a"), sems("stack_in_b")]
        max_in = sems("max_in")
        x_out = sems("x_out")
        names = ["score", "ln1T", "q", "k", "v", "oT0", "oT1", "onT", "proj", "ln2T", "mT"]
        names += [f"ffn1_{c}" for c in range(4)] + [f"ffn2_{c}" for c in range(2)]
        ready = {n: sem(n + "_ready") for n in names}
        read = {n: sem(n + "_read") for n in names}
        per_step = {n: 1 for n in names} | {"score": NSCORE}
        var1, pow1, xh1_done = sem("var1"), sem("pow1"), sem("xh1_done")
        var2, pow2, xh2_done = sem("var2"), sem("pow2"), sem("xh2_done")
        bias_scaled = sem("bias_scaled")
        rest1, mid_done, low_done = sem("rest1"), sem("mid_done"), sem("low_done")
        nmT_done = sem("nm_parts_done")
        scoresT_ready, exp_done, masked, pv_done = sem("scoresT_ready"), sem("exp_done"), sem("masked"), sem("pv_done")
        oraw_done = sems("oraw_done")
        xb_done, x1b_done = sem("xb_done"), sem("x1b_done")
        vp_init = sem("vp_init")

        def at(k, u, off):
            return 2 * k + (u + off)

        def active(k, u, off):
            return not isinstance(k, int) or 0 <= 2 * k + u + off < NSTEP

        def need(eng, s, per, n, c):
            v = n * per + c if per != 1 else n + c
            if not isinstance(v, int) or v > 0:
                eng.wait_ge(s, v)

        def need2(eng, s, per, k, u, off, back=0):
            v = k + ((u + off) // 2 + 1 - back)
            v = v * per
            if not isinstance(v, int) or v > 0:
                eng.wait_ge(s, v)

        def bank_free(eng, k, u, w):
            it = 0
            i = w - 2
            while True:
                if i < 0:
                    i += len(WORK)
                    it -= 1
                name, off, t = WORK[i]
                if isinstance(k, int) and 2 * k + u + it + 2 < 0:
                    return
                if active(k, u, off + it):
                    need(eng, read[name], per_step[name], at(k, u, off + it), 1 if t is None else t + 1)
                    return
                i -= 2

        def run(eng, body):
            for it in range(-3, 2):
                body(it // 2, it % 2)
            last = (NSTEP - 3) // 2
            with eng.Fori(1, last) as k:
                body(k, 0)
                body(k, 1)
            for it in range(2 * last, NSTEP + 1):
                body(it // 2, it % 2)

        block = ctx.enter_context(nc.Block())

        @block.sync
        def _(sp):
            for p in range(2):
                sp.dma_start(QS[p][M_ROW:P, :, :], qc_d).then_inc(const_in, 16)
                sp.dma_start(KS[p][M_ROW:P, :, :], kc_d).then_inc(const_in, 16)
            sp.dma_start(ident[:, :], id_d).then_inc(const_in, 16)
            sp.dma_start(identb[:, :], idb_d).then_inc(const_in, 16)

            def refill(k, u, g):
                n, p, hs = at(k, u, 2), u % 2, slice(8 * g, 8 * g + 8)
                for qk, stack in ((0, QS[p]), (1, KS[p])):
                    for row, part, count in ((0, 0, 3), (24, 1 if qk else 0, 2), (40, 2 if qk else 0, 1)):
                        src = scr[p][qk, part:part + count].rearrange("c (d h) t -> (c d) h t", h=H)[:, hs, :]
                        sp.dma_start(stack[row:row + 8 * count, hs, :], src).then_inc(stack_in[g][p], 16)
                sp.dma_start(QS[p][M_ROW:M_ROW + 2, hs, :], zero2[:, :].rearrange("p (h t) -> p h t", t=T)).then_inc(stack_in[g][p], 16)

            def body(k, u):
                if active(k, u, 3):
                    n, p = at(k, u, 3), (u + 3) % 2
                    need2(sp, x_out[(u - 2) % 2], 16, k, u, -2)
                    need(sp, xh1_done, 1, n, -1)
                    sp.dma_start(x_ln[p][:, :, :], xs[n].rearrange("p (b d) -> p b d", d=D)).then_inc(x_ln_in[p], 16)
                    need(sp, read["k"], 1, n, -1)
                    sp.dma_start(wqk[p][:, :], wqk_d[n // NB]).then_inc(wqk_in[p], 16)
                if active(k, u, 2):
                    n, p = at(k, u, 2), (u + 2) % 2
                    need(sp, read["v"], 1, n, -1)
                    sp.dma_start(wv[p][:, :], wv_d[n // NB]).then_inc(wv_in[p], 16)
                if active(k, u, 0):
                    n, p = at(k, u, 0), u % 2
                    need(sp, xb_done, 1, n, -1)
                    sp.dma_start(x_res[p][:, :, :], xs[n].rearrange("p (b d) -> p b d", d=D)).then_inc(x_res_in[p], 16)
                    need(sp, read["ffn2_1"], 1, n, -1)
                    need(sp, x1b_done, 1, n, -1)
                    sp.dma_start(wof[p][:, :], wof_d[n // NB]).then_inc(wof_in[p], 16)
                if active(k, u, 2):
                    n, p = at(k, u, 2), u % 2
                    need(sp, low_done, 4, n, 4)
                    for g in range(2):
                        need2(sp, stack_in[g][p], 112, k, u, 2, back=1)
                    for qk in range(2):
                        sp.dma_start(scr[p][qk].rearrange("c p t -> p c t"), parts[:, qk, :, :]).then_inc(parts_out[p], 16)
                    need2(sp, parts_out[p], 32, k, u, 2)
                    if active(k, u, 0):
                        need(sp, scoresT_ready, 32, n, -64 + 16)
                    refill(k, u, 0)
                if active(k, u, -1):
                    n, p = at(k, u, -1), (u - 1) % 2
                    need(sp, read["ffn2_1"], 1, n, 1)
                    sp.dma_start(xs[n + NB].rearrange("p (b d) -> p b d", d=D), xo[p][:, :, :]).then_inc(x_out[p], 16)
                if active(k, u, 1):
                    n, p = at(k, u, 1), (u + 1) % 2
                    need(sp, read["mT"], 1, n, 1)
                    for c in range(2):
                        sp.dma_start(QS[p][M_ROW + c:M_ROW + c + 1, :, :].rearrange("c h (i q) -> c (h i) q", q=P),
                                     nmT[64 * c:64 * c + 64, :]).then_inc(max_in[p], 16)
                if active(k, u, 2):
                    n = at(k, u, 2)
                    if active(k, u, 0):
                        need(sp, scoresT_ready, 32, n, -64 + 32)
                    refill(k, u, 1)

            run(sp, body)
            for p in range(2):
                sp.wait_ge(x_out[p], 16 * (NSTEP // 2))

        @block.tensor
        def _(pe):
            pe.wait_ge(const_in, 16 * 6)
            pe.wait_ge(vp_init, 2)

            def scores_for_exp(k, u, s):
                r, j = s // 4, s % 4
                p = u % 2
                if s == 0:
                    need2(pe, max_in[p], 32, k, u, 0)
                for v in range(2):
                    need(pe, exp_done, 32, at(k, u, 0), 2 * s + v + 1 - 2)
                    for a in range(2):
                        h = 4 * r + 2 * v + a
                        for rows, q0, q1 in ((KSTEP, j * P, (j + 1) * P), (KROW, (j + 1) * P, T)):
                            if q1 > q0:
                                last = nc.tensor.matmul(ST[v][:, a, q0 - j * P:q1 - j * P], KS[p][0:rows, h, j * P:(j + 1) * P],
                                                        QS[p][0:rows, h, q0:q1], start=True, stop=True)
                    last.then_inc(scoresT_ready, 1)

            def weighted_values(k, u, off, s):
                r, j = s // 4, s % 4
                p = (u + off) % 2
                n = at(k, u, off)
                need(pe, masked, 16, n, s + 1)
                if s == 0:
                    need(pe, oraw_done[0], 1, n, 0)
                    need(pe, read["v"], 1, n, 1)
                if s == 12:
                    need(pe, oraw_done[1], 1, n, 0)
                for a in range(4):
                    last = nc.tensor.matmul(PV[r // 3][32 * a:32 * a + 32, j * P:T], Vp[p][:, j, 4 * r + a, :],
                                            PT[:, j, a, 0:T - j * P], start=(s in (0, 12)), stop=(s in (11, 15)))
                last.then_inc(pv_done, 1)

            def work(k, u, w):
                name, off, t = WORK[w]
                n, p, out = at(k, u, off), (u + off) % 2, W[w % 2]
                bank_free(pe, k, u, w)
                if name == "score":
                    quad, (i, heads) = t // len(SCORE_TILES), SCORE_TILES[t % len(SCORE_TILES)]
                    if t == 0:
                        need2(pe, stack_in[0][p], 112, k, u, off)
                    if t == 2 * len(SCORE_TILES):
                        need2(pe, stack_in[1][p], 112, k, u, off)
                    width = (i + 1) * P
                    for m, a in enumerate(heads):
                        h = 4 * quad + a
                        for rows, k0, k1 in ((KROW, 0, i * P), (P, i * P, width)):
                            if k1 > k0:
                                last = nc.tensor.matmul(out[:, m * width + k0:m * width + k1], QS[p][0:rows, h, i * P:(i + 1) * P],
                                                        KS[p][0:rows, h, k0:k1], start=True, stop=True)
                elif name == "ln1T":
                    need(pe, xh1_done, 1, n, 1)
                    for b in range(TB):
                        last = nc.tensor.transpose(out[:, b * P:(b + 1) * P], xh1[:, b, :], ident[:, :])
                elif name in ("q", "k"):
                    need(pe, read["ln1T"], 1, n, 1)
                    need2(pe, wqk_in[p], 16, k, u, off)
                    c = D * (name == "k")
                    last = nc.tensor.matmul(out[:, :], wqk[p][:, c:c + D], xnT[p][:, :], start=True, stop=True)
                elif name == "v":
                    need2(pe, wv_in[p], 16, k, u, off)
                    for b in range(TB):
                        last = nc.tensor.matmul(out[:, b * P:(b + 1) * P], xnT[p][:, b * P:(b + 1) * P], wv[p][:, 0:D],
                                                start=True, stop=True)
                elif name in ("oT0", "oT1"):
                    c = int(name[-1])
                    need(pe, oraw_done[c], 1, n, 1)
                    for b in range(TB):
                        last = nc.tensor.transpose(out[:, b * P:(b + 1) * P], oraw[:, c, b * P:(b + 1) * P], ident[:, :])
                elif name == "onT":
                    need(pe, read["oT1"], 1, n, 1)
                    for b in range(TB):
                        last = nc.tensor.transpose(out[:, b * P:(b + 1) * P], on[:, b, :, :].rearrange("p h d -> p (h d)"), ident[:, :])
                elif name == "proj":
                    need(pe, read["onT"], 1, n, 1)
                    need2(pe, wof_in[p], 16, k, u, off)
                    for b in range(TB):
                        last = nc.tensor.matmul(out[:, b * P:(b + 1) * P], onT[:, b * P:(b + 1) * P], wof[p][:, 0:D], start=True, stop=True)
                elif name == "ln2T":
                    need(pe, xh2_done, 1, n, 1)
                    for b in range(TB):
                        last = nc.tensor.transpose(out[:, b * P:(b + 1) * P], xh2[:, b, :], ident[:, :])
                elif name[:5] == "ffn1_":
                    c = int(name[-1])
                    need(pe, read["ln2T"], 1, n, 1)
                    last = nc.tensor.matmul(out[:, :], wof[p][:, (2 + c) * D:(3 + c) * D], xnT2[:, :], start=True, stop=True)
                elif name[:5] == "ffn2_":
                    g = int(name[-1])
                    need(pe, read["ffn1_3"], 1, n, 1)
                    for b in range(2):
                        for c in range(4):
                            last = nc.tensor.matmul(out[:, b * P:(b + 1) * P], hT[:, c, (2 * g + b) * P:(2 * g + b + 1) * P],
                                                    wof[p][:, (6 + c) * D:(7 + c) * D], start=(c == 0), stop=(c == 3))
                else:
                    need(pe, nmT_done, 1, n, 1)
                    last = nc.tensor.transpose(out[:, :].bitcast(BF16)[:, 0:P], nm_p[:, :, :, :].rearrange("p c h i -> p (c h i)"), identb[:, :])
                last.then_inc(ready[name], 1)

            def body(k, u):
                w = 0
                for s in range(16):
                    if active(k, u, 0):
                        scores_for_exp(k, u, s)
                    for _ in range(len(SCORES[s]) + len(MISC.get(s, []))):
                        if active(k, u, WORK[w][1]):
                            work(k, u, w)
                        w += 1
                    off, back = (0, s - 2) if s >= 2 else (-1, s + 14)
                    if active(k, u, off):
                        weighted_values(k, u, off, back)

            run(pe, body)

        @block.scalar
        def _(act):
            def exps(k, u, s):
                r, j = s // 4, s % 4
                width = T - j * P
                n = at(k, u, 0)
                need(act, pv_done, 16, n, s + 1 - 4)
                for v in range(2):
                    need(act, scoresT_ready, 32, n, 2 * s + v + 1)
                    nc.scalar.activation(PT[:, j, 2 * v:2 * v + 2, 0:width], ST[v][:, :, 0:width], ACT.Exp).then_inc(exp_done, 1)

            def copy_sums(k, u, off, c):
                n = at(k, u, off)
                need(act, pv_done, 16, n, 16 if c else 12)
                need(act, ready[f"oT{c}"], 1, n, 0)
                nc.scalar.activation(oraw[:, c, :], PV[c][:, :], ACT.Copy).then_inc(oraw_done[c], 1)

            def work(k, u, w):
                name, off, t = WORK[w]
                n, p, src = at(k, u, off), (u + off) % 2, W[w % 2]
                if name == "ln1T":
                    need(act, ready["ln1T"], 1, n, 1)
                    need2(act, wqk_in[p], 16, k, u, off)
                    need(act, read["v"], 1, n, -1)
                    nc.scalar.activation(xnT[p][:, :], src[:, :], ACT.Identity, bias=wqk[p][:, 2 * D + 1:2 * D + 2],
                                         scale=wqk[p][:, 2 * D:2 * D + 1]).then_inc(read["ln1T"], 1)
                elif name in ("q", "k"):
                    i = int(name == "k")
                    need(act, ready[name], 1, n, 1)
                    bias, scale = (wqk[p][:, 2 * D + 3:2 * D + 4], 1.0) if i else (bqk_s[:, 0:1], 1.0 / math.sqrt(HD))
                    if not i:
                        need(act, bias_scaled, 1, n, 1)
                    need(act, rest1, 2, n, i - 1)
                    need2(act, parts_out[(p + 1) % 2], 32, k, u, off - 1)
                    nc.scalar.activation(parts[:, i, 2 * i, :], src[:, :], ACT.Identity, bias=bias, scale=scale)
                    nc.scalar.activation(qk32[:, i, :], src[:, :], ACT.Identity, bias=bias, scale=scale).then_inc(read[name], 1)
                elif name == "onT":
                    need(act, ready["onT"], 1, n, 1)
                    need(act, ready["proj"], 1, n, 0)
                    nc.scalar.activation(onT[:, :], src[:, :], ACT.Copy).then_inc(read["onT"], 1)
                elif name == "ln2T":
                    need(act, ready["ln2T"], 1, n, 1)
                    need(act, ready["ffn1_3"], 1, n, 0)
                    nc.scalar.activation(xnT2[:, :], src[:, :], ACT.Identity, bias=wof[p][:, 11 * D + 1:11 * D + 2],
                                         scale=wof[p][:, 11 * D:11 * D + 1]).then_inc(read["ln2T"], 1)
                elif name[:5] == "ffn1_":
                    c = int(name[-1])
                    need(act, ready[name], 1, n, 1)
                    if c == 0:
                        need(act, ready["ffn2_1"], 1, n, 0)
                    nc.scalar.activation(hT[:, c, :], src[:, :], ACT.Gelu,
                                         bias=wof[p][:, 11 * D + 2 + c:11 * D + 3 + c]).then_inc(read[name], 1)

            def middle_parts(k, u, i):
                n = at(k, u, 2)
                need(act, rest1, 2, n, i + 1)
                nc.scalar.activation(parts[:, i, 1, :], qk_r[:, i, :], ACT.Copy).then_inc(mid_done, 1)

            def body(k, u):
                w = 0
                for s in range(16):
                    if active(k, u, 0):
                        exps(k, u, s)
                    if s == 2 and active(k, u, -1):
                        copy_sums(k, u, -1, 1)
                    if s == 14 and active(k, u, 0):
                        copy_sums(k, u, 0, 0)
                    for _ in range(len(SCORES[s]) + len(MISC.get(s, []))):
                        if active(k, u, WORK[w][1]):
                            work(k, u, w)
                        w += 1
                    if s in (5, 6) and active(k, u, 2):
                        middle_parts(k, u, s - 5)

            run(act, body)

        @block.vector
        def _(dve):
            nc.vector.memset(nhalf[:, :], -0.5)
            nc.vector.memset(qscale[:, :], 1.0 / math.sqrt(HD))
            nc.vector.memset(zero2[:, :], 0.0)
            for p in range(2):
                nc.vector.memset(Vp[p][:, :, :, :].rearrange("p b h c -> p (b h c)"), 0.0)
            dve.drain()
            for p in range(2):
                for r in range(QUADS):
                    c = 24 + r % 3
                    last = nc.vector.memset(Vp[p][:, :, 4 * r:4 * r + 4, c:c + 1], 1.0)
                last.then_inc(vp_init, 1)

            def stats(src, st, mv, done):
                for b in range(TB):
                    nc.vector.bn_stats(st[:, b, :], src[:, b, :])
                dve.drain()
                for b in range(TB):
                    nc.vector.bn_aggr(mv[:, b, :], st[:, b, :])
                dve.drain()
                nc.vector.tensor_scalar(mv[:, :, 1], mv[:, :, 1], EPS, None, ALU.add).then_inc(done, 1)

            def standardise(src, mv, rs, dst, done):
                for b in range(TB):
                    last = nc.vector.tensor_scalar(dst[:, b, :], src[:, b, :], mv[:, b, 0:1], rs[:, b:b + 1], ALU.subtract, ALU.mult)
                last.then_inc(done, 1)

            def work(k, u, w):
                name, off, t = WORK[w]
                n, p, src = at(k, u, off), (u + off) % 2, W[w % 2]
                if name == "score":
                    quad, (i, heads) = t // len(SCORE_TILES), SCORE_TILES[t % len(SCORE_TILES)]
                    h = 4 * quad + heads[0]
                    need(dve, ready["score"], NSCORE, n, t + 1)
                    nc.vector.tensor_reduce(nmax[:, h:h + len(heads), i], src[:, 0:len(heads) * (i + 1) * P].rearrange(
                        "p (h c) -> p h c", h=len(heads)), AX.X, ALU.max, negate=True).then_inc(read["score"], 1)
                elif name == "v":
                    need(dve, ready["v"], 1, n, 1)
                    need2(dve, wv_in[p], 16, k, u, off)
                    need(dve, pv_done, 16, n, -16)
                    for r in range(QUADS):
                        c = 8 * (r % 3)
                        bv = wv[p][:, D + 32 * r:D + 32 * r + 32].rearrange("p (a d) -> p a d", d=HD)
                        last = nc.vector.tensor_tensor(
                            Vp[p][:, :, 4 * r:4 * r + 4, c:c + HD],
                            src[:, :].rearrange("p (b h d) -> p b h d", b=TB, d=HD)[:, :, 4 * r:4 * r + 4, :],
                            bv.unsqueeze(1).to_broadcast([P, TB, 4, HD]), ALU.add)
                    last.then_inc(read["v"], 1)
                elif name in ("oT0", "oT1"):
                    c = int(name[-1])
                    need(dve, ready[name], 1, n, 1)
                    if c == 0:
                        need(dve, ready["onT"], 1, n, 0)
                    tile = src[:, :].rearrange("p (b a c) -> p b a c", b=TB, a=4)
                    rs = range(3) if c == 0 else (3,)
                    for r in rs:
                        nc.vector.reciprocal(rsum[:, :, 4 * r:4 * r + 4], tile[:, :, :, 24 + r % 3])
                    dve.drain()
                    for r in rs:
                        last = nc.vector.tensor_tensor(on[:, :, 4 * r:4 * r + 4, :], tile[:, :, :, 8 * (r % 3):8 * (r % 3) + 8],
                                                       rsum[:, :, 4 * r:4 * r + 4].unsqueeze(3).to_broadcast([P, TB, 4, HD]), ALU.mult)
                    last.then_inc(read[name], 1)
                elif name == "proj":
                    need(dve, ready["proj"], 1, n, 1)
                    need(dve, xb_done, 1, n, 1)
                    need(dve, x1b_done, 1, n, 0)
                    nc.vector.tensor_tensor(x1[:, :, :], src[:, :].rearrange("p (b d) -> p b d", b=TB), xb[:, :, :], ALU.add).then_inc(read["proj"], 1)
                    dve.drain()
                    stats(x1, st2, mv2, var2)
                elif name[:5] == "ffn2_":
                    g = int(name[-1])
                    need(dve, ready[name], 1, n, 1)
                    need(dve, x1b_done, 1, n, 1)
                    if g == 0:
                        need2(dve, x_out[p], 16, k, u, off, back=1)
                    nc.vector.tensor_tensor(xo[p][:, 2 * g:2 * g + 2, :], src[:, 0:2 * P].rearrange("p (b d) -> p b d", b=2),
                                            x1b[:, 2 * g:2 * g + 2, :], ALU.add).then_inc(read[name], 1)
                elif name == "mT":
                    need(dve, ready["mT"], 1, n, 1)
                    need2(dve, max_in[(p + 1) % 2], 32, k, u, off - 1)
                    nc.vector.tensor_copy(nmT[:, :], src[:, :].bitcast(BF16)[:, 0:P]).then_inc(read["mT"], 1)

            def body(k, u):
                w = 0
                for s in range(16):
                    if s == 0 and active(k, u, 2):
                        p = u % 2
                        need2(dve, x_ln_in[p], 16, k, u, 2)
                        stats(x_ln[p], st1, mv1, var1)
                    if s == 9 and active(k, u, -1):
                        n = at(k, u, -1)
                        need(dve, pow2, 1, n, 1)
                        need(dve, ready["ln2T"], 1, n, 0)
                        standardise(x1, mv2, rs2, xh2, xh2_done)
                    if s == 2 and active(k, u, 2):
                        n, p = at(k, u, 2), u % 2
                        need(dve, pow1, 1, n, 1)
                        need(dve, ready["ln1T"], 1, n, 0)
                        standardise(x_ln[p], mv1, rs1, xh1, xh1_done)
                    if s == 14 and active(k, u, 1):
                        n = at(k, u, 1)
                        dve.drain()
                        need(dve, ready["mT"], 1, n, 0)
                        nc.vector.tensor_copy(nm_p[:, 0, :, :], nmax[:, :, :])
                        dve.drain()
                        nc.vector.tensor_tensor(nm_p[:, 1, :, :], nmax[:, :, :], nm_p[:, 0, :, :], ALU.subtract).then_inc(nmT_done, 1)
                    for _ in range(len(SCORES[s]) + len(MISC.get(s, []))):
                        if active(k, u, WORK[w][1]):
                            work(k, u, w)
                        w += 1

            run(dve, body)

        @block.gpsimd
        def _(pool):
            nc.gpsimd.memset(word[:, :], 0.0)

            def rest(k, u, i):
                n = at(k, u, 2)
                need(pool, read["k" if i else "q"], 1, n, 1)
                nc.gpsimd.tensor_tensor(qk_r[:, i, :], qk32[:, i, :], parts[:, i, 2 * i, :], ALU.subtract).then_inc(rest1, 1)

            def low(k, u, i):
                n = at(k, u, 2)
                need(pool, mid_done, 2, n, i + 1)
                nc.gpsimd.tensor_tensor(parts[:, i, 2 - 2 * i, :], qk_r[:, i, :], parts[:, i, 1, :], ALU.subtract).then_inc(low_done, 2)

            def body(k, u):
                for s in range(16):
                    if active(k, u, 0):
                        n, j = at(k, u, 0), s % 4
                        need(pool, exp_done, 32, n, 2 * s + 2)
                        nc.gpsimd.tensor_tensor(word[:, 1 + s:2 + s], word[:, 0:1], word[:, 0:1], ALU.add)
                        blk = PT[:, j, :, 0:P]
                        nc.gpsimd.affine_select(out=blk, in_=blk, pattern=[[0, 4], [1, P]], compare_op=ALU.is_ge, fill=0.0,
                                                base=0, channel_multiplier=-1).then_inc(masked, 1)
                    if s == 0 and active(k, u, 2):
                        n, p = at(k, u, 2), u % 2
                        need(pool, var1, 1, n, 1)
                        need(pool, xh1_done, 1, n, 0)
                        nc.gpsimd.tensor_tensor(rs1[:, :], mv1[:, :, 1], nhalf[:, :], ALU.pow).then_inc(pow1, 1)
                        need2(pool, wqk_in[p], 16, k, u, 2)
                        need(pool, read["q"], 1, n, 0)
                        nc.gpsimd.tensor_tensor(bqk_s[:, :], wqk[p][:, 2 * D + 2:2 * D + 3], qscale[:, :], ALU.mult).then_inc(bias_scaled, 1)
                    if s == 1 and active(k, u, -1):
                        n, p = at(k, u, -1), (u - 1) % 2
                        need2(pool, x_res_in[p], 16, k, u, -1)
                        need2(pool, wof_in[p], 16, k, u, -1)
                        need(pool, read["proj"], 1, n, 0)
                        nc.gpsimd.tensor_tensor(xb[:, :, :], x_res[p][:, :, :], wof[p][:, D:2 * D].unsqueeze(1).to_broadcast([P, TB, D]),
                                                ALU.add).then_inc(xb_done, 1)
                    if s == 8 and active(k, u, -1):
                        n, p = at(k, u, -1), (u - 1) % 2
                        need(pool, var2, 1, n, 1)
                        need(pool, xh2_done, 1, n, 0)
                        nc.gpsimd.tensor_tensor(rs2[:, :], mv2[:, :, 1], nhalf[:, :], ALU.pow).then_inc(pow2, 1)
                        need(pool, read["ffn2_1"], 1, n, 0)
                        nc.gpsimd.tensor_tensor(x1b[:, :, :], x1[:, :, :], wof[p][:, 10 * D:11 * D].unsqueeze(1).to_broadcast([P, TB, D]),
                                                ALU.add).then_inc(x1b_done, 1)
                    if active(k, u, 2):
                        if s == 4:
                            rest(k, u, 0)
                        if s == 5:
                            rest(k, u, 1)
                        if s == 6:
                            low(k, u, 0)
                        if s == 7:
                            low(k, u, 1)

            run(pool, body)


def modulation_program(nc, NB, T, io):
    TB = T // P
    NM = 6 * D
    with ExitStack() as ctx:
        def sb(name, shape, dt=F32):
            return ctx.enter_context(nc.sbuf_tensor(name, shape, dt))

        def sem(name):
            return ctx.enter_context(nc.semaphore(name))

        cT = sb("cT", [P, NB])
        scT = sb("scT", [P, NB])
        wmod = sb("wmod", [P, NM])
        mod = sb("mod", [NB, 6, D])
        gate_abs = sb("gate_abs", [NB, 2, D])
        gate_sign = sb("gate_sign", [NB, 2, D])
        x0 = [sb(f"x0_{i}", [P, TB, D]) for i in range(2)]
        rows = [sb(f"mod_rows{i}", [P, 2, D]) for i in range(2)]
        st = sb("st0", [P, TB, 6])
        mv = sb("mv0", [P, TB, 2])
        rs = sb("rs0", [P, TB])
        nh = sb("nhalf0", [P, TB])
        xh = sb("xh0", [P, TB, D])
        hm = sb("hm0", [P, TB, D])
        h = [sb(f"h0_{i}", [P, TB, D]) for i in range(2)]
        pm = ctx.enter_context(nc.psum_tensor("mod_ps", [NB, 2, 512], F32))
        c_in, silu_done, mod_ready, mod_done, mod_out = (sem(n) for n in ("c_in", "silu_done", "mod_ready", "mod_done", "mod_out"))
        x0_in = [sem(f"x0_in{i}") for i in range(2)]
        h_out = [sem(f"h_out{i}") for i in range(2)]
        var_done, pow_done, h_done = sem("var0"), sem("pow0"), sem("h0_done")
        block = ctx.enter_context(nc.Block())

        @block.sync
        def _(sp):
            sp.dma_start(cT[:, :], io["cT"]).then_inc(c_in, 16)
            sp.dma_start(wmod[:, :], io["wmod"]).then_inc(c_in, 16)
            sp.wait_ge(mod_done, 1)
            sp.dma_start(io["mod"], mod[:, :, :].rearrange("b c d -> b (c d)")).then_inc(mod_out, 16)
            sp.wait_ge(mod_out, 16)

            def load(k, u, b):
                sp.dma_start(x0[u][:, :, :], io["x"][b].rearrange("(t p) d -> p t d", p=P)).then_inc(x0_in[u], 16)
                sp.dma_start(rows[u][:, :, :].rearrange("p c d -> p (c d)"), io["mod"][b, 0:2 * D].partition_broadcast(P)).then_inc(x0_in[u], 16)

            def store(k, u, b):
                sp.wait_ge(h_done, b + 1)
                sp.dma_start(io["xs"][b].rearrange("p (t d) -> p t d", d=D), h[u][:, :, :]).then_inc(h_out[u], 16)

            load(0, 0, 0)
            load(0, 1, 1)
            with sp.Fori(0, NB // 2 - 1) as k:
                for u in range(2):
                    store(k, u, 2 * k + u)
                    load(k, u, 2 * k + u + 2)
            for u in range(2):
                store(NB // 2 - 1, u, NB - 2 + u)
            for u in range(2):
                sp.wait_ge(h_out[u], 16 * (NB // 2))

        @block.scalar
        def _(act):
            act.wait_ge(c_in, 32)
            nc.scalar.activation(scT[:, :], cT[:, :], ACT.Silu).then_inc(silu_done, 1)

        @block.tensor
        def _(pe):
            pe.wait_ge(silu_done, 1)
            for i in range(2):
                last = nc.tensor.matmul(pm[:, i, 0:NM // 2], scT[:, :], wmod[:, i * NM // 2:(i + 1) * NM // 2], start=True, stop=True)
            last.then_inc(mod_ready, 1)

        @block.vector
        def _(dve):
            dve.wait_ge(mod_ready, 1)
            for i in range(2):
                nc.vector.tensor_copy(mod[:, 3 * i:3 * i + 3, :].rearrange("b c d -> b (c d)"), pm[:, i, 0:NM // 2])
            nc.vector.memset(nh[:, :], -0.5)
            dve.drain()
            both = mod[:, :, :].rearrange("b (i c) d -> b i c d", c=3)
            nc.vector.tensor_scalar(gate_sign[:, :, :], both[:, :, 2, :], 0.0, 2.0, ALU.is_ge, ALU.mult)
            nc.vector.scalar_tensor_tensor(out=gate_abs[:, :, :], in0=both[:, :, 2, :], scalar=-1.0, in1=both[:, :, 2, :],
                                           op0=ALU.mult, op1=ALU.max)
            nc.vector.tensor_scalar(both[:, :, 1, :], both[:, :, 1, :], 1.0, None, ALU.add)
            dve.drain()
            nc.vector.tensor_scalar(gate_abs[:, :, :], gate_abs[:, :, :], 0.25, None, ALU.max)
            dve.drain()
            nc.vector.scalar_tensor_tensor(out=both[:, :, 2, :], in0=gate_sign[:, :, :], scalar=-1.0, in1=gate_abs[:, :, :],
                                           op0=ALU.add, op1=ALU.mult).then_inc(mod_done, 1)

            def sequence(k, u):
                    b = 2 * k + u
                    dve.wait_ge(x0_in[u], 32 * k + 32)
                    for t in range(TB):
                        nc.vector.bn_stats(st[:, t, :], x0[u][:, t, :])
                    dve.drain()
                    for t in range(TB):
                        nc.vector.bn_aggr(mv[:, t, :], st[:, t, :])
                    dve.drain()
                    nc.vector.tensor_scalar(mv[:, :, 1], mv[:, :, 1], EPS, None, ALU.add).then_inc(var_done, 1)
                    dve.wait_ge(pow_done, b + 1)
                    for t in range(TB):
                        nc.vector.tensor_scalar(xh[:, t, :], x0[u][:, t, :], mv[:, t, 0:1], rs[:, t:t + 1], ALU.subtract, ALU.mult)
                    dve.drain()
                    nc.vector.tensor_tensor(hm[:, :, :], xh[:, :, :], rows[u][:, 1:2, :].to_broadcast([P, TB, D]), ALU.mult)
                    dve.drain()
                    if not isinstance(k, int):
                        dve.wait_ge(h_out[u], 16 * k)
                    nc.vector.tensor_tensor(h[u][:, :, :], hm[:, :, :], rows[u][:, 0:1, :].to_broadcast([P, TB, D]), ALU.add).then_inc(h_done, 1)

            sequence(0, 0)
            sequence(0, 1)
            with dve.Fori(1, NB // 2) as k:
                sequence(k, 0)
                sequence(k, 1)

        @block.gpsimd
        def _(pool):
            with pool.Fori(0, NB // 2) as k:
                for u in range(2):
                    pool.wait_ge(var_done, 2 * k + u + 1)
                    nc.gpsimd.tensor_tensor(rs[:, :], mv[:, :, 1], nh[:, :], ALU.pow).then_inc(pow_done, 1)


def experts_program(nc, NB, L, T, io):
    TB = T // P
    NM = 6 * D
    with ExitStack() as ctx:
        def sb(name, shape, dt=F32):
            return ctx.enter_context(nc.sbuf_tensor(name, shape, dt))

        def two(name, shape, dt=F32):
            return [sb(f"{name}{i}", shape, dt) for i in range(2)]

        def ps(name, shape):
            return ctx.enter_context(nc.psum_tensor(name, shape, F32))

        def sem(name):
            return ctx.enter_context(nc.semaphore(name))

        y = two("y_rows", [P, TB, D])
        x0 = two("x_rows", [P, TB, D])
        rows = two("mod_rows_e", [P, 6, D])
        fin = sb("final_wb", [P, 2, D])
        gate_w = sb("gate_w", [P, E])
        w1 = sb("w1_e", [P, E, EH * P])
        b1 = sb("b1_e", [P, E * EH])
        w2 = sb("w2_e", [P, E, EH, D])
        b2 = sb("b2_e", [E, D])
        rank = sb("rank", [P, E])
        ident = sb("ident_e", [P, P])
        nh = sb("nhalf_e", [P, TB])
        st, mv, rs = sb("st_e", [P, TB, 6]), sb("mv_e", [P, TB, 2]), sb("rs_e", [P, TB])
        xh = sb("xh_e", [P, TB, D])
        g12 = sb("g12", [P, 2, D])
        xg = sb("x_plus_gfb", [P, TB, D])
        yg = sb("y_times_gfw", [P, TB, D])
        x1 = two("x1_e", [P, TB, D])
        h2a = sb("h2a", [P, TB, D])
        h2 = sb("h2", [P, TB, D])
        h2T = two("h2T", [P, T])
        lg, ex, pr, p2, eq, wr, oh1, oh2 = (sb(n, [P, TB, E]) for n in ("lg", "ex", "pr", "p2", "eq", "wr", "oh1", "oh2"))
        mx, sm, rc = (sb(n, [P, TB]) for n in ("mx", "sm", "rc"))
        gt = two("gates", [P, TB, E])
        gT = two("gatesT", [E, T])
        hs = two("hidden", [P, EH, T])
        acc = sb("acc", [P, TB, D])
        accg = sb("acc_gated", [P, TB, D])
        out = two("out_rows", [P, TB, D])
        hp = [ps(f"hidden_ps{i}", [P, EH, T]) for i in range(2)]
        op = [ps(f"expert_ps{i}", [P, TB, D]) for i in range(2)]
        tp = ps("transposed_ps", [P, T])
        gp = ps("router_ps", [P, T])

        w_in = sem("w_in")
        y_in, out_out = [sem(f"y_in{i}") for i in range(2)], [sem(f"out_out{i}") for i in range(2)]
        (init_done, var_done, pow_done, g12_done, xg_done, x1_done, h2_done, h2T_ready, h2T_done, lg_ready, lg_done, ex_done,
         gates_done, gT_ready, gT_done, b2_ready, b2_read, hid_ready, hid_done, exp_ready, exp_read, out_done) = (
            sem("e_" + n) for n in ("init_done", "var_done", "pow_done", "g12_done", "xg_done", "x1_done", "h2_done", "h2T_ready",
                                    "h2T_done", "lg_ready", "lg_done", "ex_done", "gates_done", "gT_ready", "gT_done", "b2_ready",
                                    "b2_read", "hid_ready", "hid_done", "exp_ready", "exp_read", "out_done"))

        def need(eng, s, v):
            if not isinstance(v, int) or v > 0:
                eng.wait_ge(s, v)

        def run(eng, first, pair):
            first()
            for u in range(2):
                pair(0, u, True)
            with eng.Fori(1, NB // 2 - 1) as k:
                for u in range(2):
                    pair(k, u, True)
            for u in range(2):
                pair(NB // 2 - 1, u, u == 0)

        block = ctx.enter_context(nc.Block())

        @block.sync
        def _(sp):
            for dst, src in ((fin[:, :, :].rearrange("p c d -> p (c d)"), io["final"].partition_broadcast(P)), (gate_w[:, :], io["gate"]),
                             (rank[:, :], io["rank"].partition_broadcast(P)), (ident[:, :], io["ident"]), (b1[:, :], io["b1"]), (b2[:, :], io["b2"]),
                             (w1[:, :, :], io["w1"].rearrange("e d h -> d e h")),
                             (w2[:, :, :, :].rearrange("p e c d -> p (e c) d"), io["w2"].rearrange("e (c p) d -> p (e c) d", p=P))):
                sp.dma_start(dst, src).then_inc(w_in, 16)

            def load(b, u):
                sp.dma_start(y[u][:, :, :], io["xs"][L * NB + b].rearrange("p (t d) -> p t d", d=D)).then_inc(y_in[u], 16)
                sp.dma_start(x0[u][:, :, :], io["x"][b].rearrange("(t p) d -> p t d", p=P)).then_inc(y_in[u], 16)
                sp.dma_start(rows[u][:, :, :].rearrange("p c d -> p (c d)"), io["mod"][b].partition_broadcast(P)).then_inc(y_in[u], 16)

            def pair(k, u, more):
                b = 2 * k + u
                sp.wait_ge(out_done, b + 1)
                sp.dma_start(io["out"][b].rearrange("(t p) d -> p t d", p=P), out[u][:, :, :]).then_inc(out_out[u], 16)
                if not isinstance(k, int) or b + 2 < NB:
                    load(b + 2, u)

            def first():
                load(0, 0)
                load(1, 1)

            run(sp, first, pair)
            for u in range(2):
                sp.wait_ge(out_out[u], 16 * (NB // 2))

        @block.tensor
        def _(pe):
            def up(b, u, e):
                need(pe, hid_done, 2 * (8 * b + e + 1) - 4)
                if e == 0:
                    pe.wait_ge(h2T_done, b + 1)
                for c in range(EH):
                    last = nc.tensor.matmul(hp[e % 2][:, c, :], w1[:, e, c * P:(c + 1) * P], h2T[u][:, :], start=True, stop=True)
                last.then_inc(hid_ready, 1)

            def down(b, e):
                pe.wait_ge(hid_done, 2 * (8 * b + e + 1))
                need(pe, exp_read, 8 * b + e - 1)
                for t in range(TB):
                    for c in range(EH):
                        last = nc.tensor.matmul(op[e % 2][:, t, :], hs[e % 2][:, c, t * P:(t + 1) * P], w2[:, e, c, :],
                                                start=(c == 0), stop=(c == EH - 1))
                last.then_inc(exp_ready, 1)

            def transposes(b):
                pe.wait_ge(h2_done, b + 1)
                need(pe, h2T_done, b)
                for t in range(TB):
                    last = nc.tensor.transpose(tp[:, t * P:(t + 1) * P], h2[:, t, :], ident[:, :])
                last.then_inc(h2T_ready, 1)

            def router(b, u):
                pe.wait_ge(h2T_done, b + 1)
                need(pe, b2_read, b)
                for t in range(TB):
                    last = nc.tensor.matmul(gp[:, t * E:(t + 1) * E], h2T[u][:, t * P:(t + 1) * P], gate_w[:, :], start=True, stop=True)
                last.then_inc(lg_ready, 1)

            def gates_transposed(b, u):
                pe.wait_ge(gates_done, b + 1)
                for t in range(TB):
                    last = nc.tensor.transpose(gp[0:E, t * P:(t + 1) * P], gt[u][:, t, :], ident[:, :])
                last.then_inc(gT_ready, 1)

            def first():
                pe.wait_ge(w_in, 16 * 8)
                transposes(0)
                router(0, 0)
                gates_transposed(0, 0)

            def pair(k, u, more):
                b = 2 * k + u
                pe.wait_ge(gT_done, b + 1)
                for t in range(TB):
                    last = nc.tensor.matmul(gp[:, t * P:(t + 1) * P], gT[u][:, t * P:(t + 1) * P], b2[:, :], start=True, stop=True)
                last.then_inc(b2_ready, 1)
                up(b, u, 0)
                for e in range(E):
                    if e + 1 < E:
                        up(b, u, e + 1)
                    down(b, e)
                    if more and e == 4:
                        transposes(b + 1)
                    if more and e == 5:
                        router(b + 1, 1 - u)
                if more:
                    gates_transposed(b + 1, 1 - u)

            run(pe, first, pair)

        @block.scalar
        def _(act):
            def transposed(b, u):
                act.wait_ge(h2T_ready, b + 1)
                need(act, hid_ready, 8 * b - 8)
                nc.scalar.activation(h2T[u][:, :], tp[:, :], ACT.Copy).then_inc(h2T_done, 1)

            def router(b, u):
                act.wait_ge(lg_done, b + 1)
                nc.scalar.activation(ex[:, :, :], lg[:, :, :], ACT.Exp).then_inc(ex_done, 1)

            def gates(b, u):
                act.wait_ge(gT_ready, b + 1)
                need(act, b2_ready, b - 1)
                nc.scalar.activation(gT[u][:, :], gp[0:E, :], ACT.Copy).then_inc(gT_done, 1)

            def first():
                act.wait_ge(w_in, 16 * 8)
                transposed(0, 0)
                router(0, 0)
                gates(0, 0)

            def pair(k, u, more):
                b = 2 * k + u
                for e in range(E):
                    act.wait_ge(hid_ready, 8 * b + e + 1)
                    need(act, exp_ready, 8 * b + e - 1)
                    for c in range(EH):
                        nc.scalar.activation(hs[e % 2][:, c, :], hp[e % 2][:, c, :], ACT.Relu,
                                             bias=b1[:, e * EH + c:e * EH + c + 1]).then_inc(hid_done, 1)
                    if more and e == 5:
                        transposed(b + 1, 1 - u)
                    if more and e == 7:
                        router(b + 1, 1 - u)
                if more:
                    gates(b + 1, 1 - u)

            run(act, first, pair)

        @block.vector
        def _(dve):
            def stats(src):
                for t in range(TB):
                    nc.vector.bn_stats(st[:, t, :], src[:, t, :])
                dve.drain()
                for t in range(TB):
                    nc.vector.bn_aggr(mv[:, t, :], st[:, t, :])
                dve.drain()
                nc.vector.tensor_scalar(mv[:, :, 1], mv[:, :, 1], EPS, None, ALU.add).then_inc(var_done, 1)

            def standardise(src):
                for t in range(TB):
                    nc.vector.tensor_scalar(xh[:, t, :], src[:, t, :], mv[:, t, 0:1], rs[:, t:t + 1], ALU.subtract, ALU.mult)
                dve.drain()

            def by_row(u, c):
                return rows[u][:, c:c + 1, :].to_broadcast([P, TB, D])

            def over(v):
                return v[:, :].unsqueeze(2).to_broadcast([P, TB, E])

            def pre1(k, b, u, half):
                dve.wait_ge(y_in[u], 48 * half)
                stats(y[u])
                need(dve, xg_done, b)
                nc.vector.tensor_tensor(g12[:, :, :], fin[:, :, :], rows[u][:, 2:3, :].to_broadcast([P, 2, D]), ALU.mult).then_inc(g12_done, 1)

            def pre2(k, b, u):
                dve.wait_ge(pow_done, 2 * b + 1)
                standardise(y[u])
                nc.vector.tensor_tensor(yg[:, :, :], xh[:, :, :], g12[:, 0:1, :].to_broadcast([P, TB, D]), ALU.mult)
                dve.drain()
                dve.wait_ge(xg_done, b + 1)
                nc.vector.tensor_tensor(x1[u][:, :, :], yg[:, :, :], xg[:, :, :], ALU.add).then_inc(x1_done, 1)
                dve.drain()
                stats(x1[u])

            def pre3(k, b, u):
                dve.wait_ge(pow_done, 2 * b + 2)
                standardise(x1[u])
                nc.vector.tensor_tensor(h2a[:, :, :], xh[:, :, :], by_row(u, 4), ALU.mult)
                dve.drain()
                need(dve, h2T_ready, b)
                nc.vector.tensor_tensor(h2[:, :, :], h2a[:, :, :], by_row(u, 3), ALU.add).then_inc(h2_done, 1)

            def route1(b, u):
                dve.wait_ge(lg_ready, b + 1)
                z = gp[:, 0:TB * E].rearrange("p (t e) -> p t e", e=E)
                nc.vector.tensor_reduce(mx[:, :], z, AX.X, ALU.max)
                dve.drain()
                nc.vector.tensor_tensor(lg[:, :, :], z, over(mx), ALU.subtract).then_inc(lg_done, 1)

            def largest(src, dst):
                nc.vector.tensor_reduce(mx[:, :], src[:, :, :], AX.X, ALU.max)
                dve.drain()
                nc.vector.tensor_tensor(eq[:, :, :], src[:, :, :], over(mx), ALU.is_equal)
                dve.drain()
                nc.vector.tensor_tensor(wr[:, :, :], eq[:, :, :], rank[:, :].unsqueeze(1).to_broadcast([P, TB, E]), ALU.mult)
                dve.drain()
                nc.vector.tensor_reduce(sm[:, :], wr[:, :, :], AX.X, ALU.max)
                dve.drain()
                nc.vector.tensor_tensor(dst[:, :, :], wr[:, :, :], over(sm), ALU.is_equal)
                dve.drain()

            def route2(b, u):
                dve.wait_ge(ex_done, b + 1)
                nc.vector.tensor_reduce(sm[:, :], ex[:, :, :], AX.X, ALU.add)
                dve.drain()
                nc.vector.reciprocal(rc[:, :], sm[:, :])
                dve.drain()
                nc.vector.tensor_tensor(pr[:, :, :], ex[:, :, :], over(rc), ALU.mult)
                dve.drain()
                largest(pr, oh1)
                nc.vector.scalar_tensor_tensor(out=p2[:, :, :], in0=oh1[:, :, :], scalar=-4.0, in1=pr[:, :, :], op0=ALU.mult, op1=ALU.add)
                dve.drain()
                largest(p2, oh2)
                nc.vector.tensor_tensor(eq[:, :, :], oh1[:, :, :], oh2[:, :, :], ALU.add)
                dve.drain()
                nc.vector.tensor_tensor(wr[:, :, :], eq[:, :, :], pr[:, :, :], ALU.mult)
                dve.drain()
                nc.vector.tensor_reduce(sm[:, :], wr[:, :, :], AX.X, ALU.add)
                dve.drain()
                nc.vector.tensor_scalar(sm[:, :], sm[:, :], 1e-12, None, ALU.max)
                dve.drain()
                nc.vector.reciprocal(rc[:, :], sm[:, :])
                dve.drain()
                nc.vector.tensor_tensor(gt[u][:, :, :], wr[:, :, :], over(rc), ALU.mult).then_inc(gates_done, 1)

            def first():
                nc.vector.memset(nh[:, :], -0.5).then_inc(init_done, 1)
                dve.wait_ge(w_in, 16 * 8)
                pre1(0, 0, 0, 1)
                pre2(0, 0, 0)
                pre3(0, 0, 0)
                route1(0, 0)
                route2(0, 0)

            def pair(k, u, more):
                b = 2 * k + u
                dve.wait_ge(b2_ready, b + 1)
                nc.vector.tensor_copy(acc[:, :, :].rearrange("p t d -> p (t d)"), gp[:, :]).then_inc(b2_read, 1)
                dve.drain()
                for e in range(E):
                    dve.wait_ge(exp_ready, 8 * b + e + 1)
                    for t in range(TB):
                        last = nc.vector.scalar_tensor_tensor(out=acc[:, t, :], in0=op[e % 2][:, t, :], scalar=gt[u][:, t, e:e + 1],
                                                              in1=acc[:, t, :], op0=ALU.mult, op1=ALU.add)
                    last.then_inc(exp_read, 1)
                    if more and e == 0:
                        pre1(k, b + 1, 1 - u, k + u + 1)
                    if more and e == 1:
                        pre2(k, b + 1, 1 - u)
                    if more and e == 2:
                        pre3(k, b + 1, 1 - u)
                    if more and e == 6:
                        route1(b + 1, 1 - u)
                    dve.drain()
                if more:
                    route2(b + 1, 1 - u)
                nc.vector.tensor_tensor(accg[:, :, :], acc[:, :, :], by_row(u, 5), ALU.mult)
                dve.drain()
                if not isinstance(k, int) or k > 0:
                    dve.wait_ge(out_out[u], 16 * k)
                nc.vector.tensor_tensor(out[u][:, :, :], accg[:, :, :], x1[u][:, :, :], ALU.add).then_inc(out_done, 1)

            run(dve, first, pair)

        @block.gpsimd
        def _(pool):
            def prepare(b, u, half):
                pool.wait_ge(var_done, 2 * b + 1)
                nc.gpsimd.tensor_tensor(rs[:, :], mv[:, :, 1], nh[:, :], ALU.pow).then_inc(pow_done, 1)
                pool.wait_ge(g12_done, b + 1)
                pool.wait_ge(y_in[u], 48 * half)
                need(pool, x1_done, b)
                nc.gpsimd.tensor_tensor(xg[:, :, :], x0[u][:, :, :], g12[:, 1:2, :].to_broadcast([P, TB, D]), ALU.add).then_inc(xg_done, 1)
                pool.wait_ge(var_done, 2 * b + 2)
                nc.gpsimd.tensor_tensor(rs[:, :], mv[:, :, 1], nh[:, :], ALU.pow).then_inc(pow_done, 1)

            def first():
                pool.wait_ge(init_done, 1)
                prepare(0, 0, 1)

            def pair(k, u, more):
                if more:
                    prepare(2 * k + u + 1, 1 - u, k + u + 1)

            run(pool, first, pair)



def tables(T):
    bf = mybir.dt.np(BF16)
    base = 2.0 ** (-(2.0 ** (-(math.log2(H) - 3))))
    slopes = (base ** np.arange(1, H + 1)).astype(np.float32).astype(np.float64)
    qc = np.zeros((P - M_ROW, H, T), np.float64)
    kc = np.zeros((P - M_ROW, H, T), np.float64)
    t = np.arange(T)
    tt = t % P
    kc[0:2] = 1.0
    rest = slopes[:, None] * (t - T // 2)[None]
    qc[2:5] = 1.0
    for i in range(3):
        part = rest.astype(bf).astype(np.float64)
        kc[2 + i] = part
        rest = rest - part
    for r in range(P // 8 - 1):
        kc[STEP_ROW - M_ROW + r] = tt >= 8 * (r + 1)
        qc[STEP_ROW - M_ROW + r] = np.where(tt < 8 * (r + 1), -2.0 ** 17, 0.0)
    for g in range(P // 8):
        kc[GROUP_ROW - M_ROW + g] = np.where(tt // 8 == g, 2.0 ** (18 * (tt % 8) - 2.0), 0.0)
        qc[GROUP_ROW - M_ROW + g] = np.where(tt // 8 == g, -(2.0 ** (-18.0 * (tt % 8))), 0.0)
    return qc.astype(bf), kc.astype(bf)


def kernel(**inputs):
    import concourse.bacc as _bacc
    from concourse.bass_utils import run_bass_kernel_spmd as _run

    a = {k: np.asarray(v) for k, v in inputs.items()}
    x = a["L0_attn_x"]
    NB, T, _ = x.shape
    L = a["L0_attn_in_proj_w"].shape[0]

    def dmajor(w):
        return w.reshape(L, H, HD, -1).transpose(0, 2, 1, 3).reshape(L, D, -1)

    def col(v):
        return v.reshape(L, D, 1)

    def row(v):
        return np.broadcast_to(v.reshape(L, 1, D), (L, P, D))

    w_in, b_in = a["L0_attn_in_proj_w"], a["L0_attn_in_proj_b"]
    f1 = a["L0_attn_ffn1_w"]
    tr = lambda w: w.transpose(0, 2, 1)
    wqk = np.concatenate([tr(dmajor(w_in[:, 0:D])), tr(dmajor(w_in[:, D:2 * D])), col(a["L0_attn_ln1_w"]), col(a["L0_attn_ln1_b"]),
                          dmajor(b_in[:, 0:D]), dmajor(b_in[:, D:2 * D])], axis=2)
    wv = np.concatenate([tr(w_in[:, 2 * D:]), row(b_in[:, 2 * D:])], axis=2)
    wof = np.concatenate([tr(a["L0_attn_out_proj_w"]), row(a["L0_attn_out_proj_b"]), tr(f1)]
                         + [tr(a["L0_attn_ffn2_w"])[:, c * P:(c + 1) * P] for c in range(4)]
                         + [row(a["L0_attn_ffn2_b"]), col(a["L0_attn_ln2_w"]), col(a["L0_attn_ln2_b"])]
                         + [a["L0_attn_ffn1_b"].reshape(L, 4, P).transpose(0, 2, 1)], axis=2)
    qc, kc = tables(T)
    arrays = {
        "x": x, "wqk": wqk, "wv": wv, "wof": wof, "qc": qc, "kc": kc,
        "ident": np.eye(P, dtype=np.float32), "identb": np.eye(P).astype(mybir.dt.np(BF16)),
        "cT": a["L0_c"].T, "wmod": a["L0_wmod"],
        "final": np.concatenate([a["L0_attn_final_w"], a["L0_attn_final_b"]]),
        "gate": a["L0_ffn_gate"], "w1": a["L0_ffn_W1"], "w2": a["L0_ffn_W2"], "b2": a["L0_ffn_b2"],
        "b1": a["L0_ffn_b1"].reshape(E * EH, P).T, "rank": np.arange(E, 0, -1).astype(np.float32),
    }
    arrays = {k: np.ascontiguousarray(v) for k, v in arrays.items()}
    nc = _bacc.Bacc("TRN2", target_bir_lowering=False, num_devices=1)
    io = {k: nc.dram_tensor(k + "_dram", v.shape, mybir.dt.from_np(v.dtype), kind="ExternalInput").ap() for k, v in arrays.items()}
    io["out"] = nc.dram_tensor("out_dram", x.shape, F32, kind="ExternalOutput").ap()
    io["xs"] = nc.dram_tensor("residual_stream", ((L + 1) * NB, P, T // P * D), F32, kind="Internal").ap()
    io["mod"] = nc.dram_tensor("modulation", (NB, 6 * D), F32, kind="Internal").ap()
    for i in range(2):
        io[f"scr{i}"] = nc.dram_tensor(f"parts_dram{i}", (2, 3, P, T), BF16, kind="Internal").ap()
    modulation_program(nc, NB, T, io)
    transformer_program(nc, NB, L, T, io)
    experts_program(nc, NB, L, T, io)
    r = _run(nc, [{k + "_dram": v for k, v in arrays.items()}], core_ids=[0])
    return r.results[0]["out_dram"]
```

```python
import concourse.bass as bass
from concourse import mybir
from contextlib import ExitStack
import math
import numpy as np

F32 = mybir.dt.float32
BF16 = mybir.dt.bfloat16
ALU = mybir.AluOpType
ACT = mybir.ActivationFunctionType
AX = mybir.AxisListType

P = 128
D = 128
H, HD = 16, 8
QUADS = H // 4
KROW = 96
M_ROW = 6 * HD
ALIBI_ROW = M_ROW + 2
STEP_ROW = KROW
GROUP_ROW = STEP_ROW + 15
KSTEP = GROUP_ROW
EPS = 1e-5
VOCT = 32
E = 8
EH = 2

BANKS = 3

SCORE_TILES = [(0, (0, 1, 2, 3)), (1, (0, 1)), (1, (2, 3))] + [(i, (a,)) for i in (2, 3) for a in range(4)]
NSCORE = len(SCORE_TILES) * QUADS
MISC = {2: [("mT1", 0)], 3: [("oT0", -1), ("oT1", -1)], 5: [("onT", -1), ("ln1T", 2)], 6: [("q", 2)],
        7: [("proj", -1)], 8: [("k", 2)], 9: [("v", 1)], 10: [("mT0", 1)], 11: [("ln2T", -1)],
        12: [("ffn1_0", -1), ("ffn1_1", -1), ("ffn1_2", -1), ("ffn1_3", -1)], 13: [("ffn2_0", -1)],
        14: [("ffn2_1", -1), ("ffn2_2", -1)], 15: [("ffn2_3", -1)]}
SCORE_COUNTS = [4, 3, 3, 2, 3, 4, 3, 2, 2, 2, 2, 2, 3, 3, 3, 3]
SCORES = [list(range(sum(SCORE_COUNTS[:s]), sum(SCORE_COUNTS[:s + 1]))) for s in range(16)]
assert len(SCORES[15]) and sum(SCORE_COUNTS) == NSCORE


def work_tiles():
    out = []
    for s in range(16):
        scores, misc = [("score", 1, t) for t in SCORES[s]], [(name, off, None) for name, off in MISC.get(s, [])]
        while scores or misc:
            out += scores[:1] + misc[:1]
            scores, misc = scores[1:], misc[1:]
    assert len(out) % BANKS == 0
    return out


WORK = work_tiles()


def pieces(s):
    count = len(SCORES[s]) + len(MISC.get(s, []))
    if MISC.get(s, [("", 0)])[0][0] == "ffn1_0":
        return (0, 0, count)
    return tuple((count + 2 - i) // 3 for i in range(3))


WQK = 2 * D + 4
WV = 2 * D
WOF = 2 * D + 4 * D + 4 * D + D + 6


def transformer_program(nc, NB, L, T, io):
    TB = T // P
    NSTEP = NB * L
    xs, wqk_d, wv_d, wof_d, qc_d, kc_d, id_d, idb_d = (io[k] for k in ("xs", "wqk", "wv", "wof", "qc", "kc", "ident", "identb"))
    scr = [io["scr0"], io["scr1"]]
    with ExitStack() as ctx:
        def sb(name, shape, dt=F32):
            return ctx.enter_context(nc.sbuf_tensor(name, shape, dt))

        def two(name, shape, dt=F32):
            return [sb(f"{name}{i}", shape, dt) for i in range(2)]

        def sem(name):
            return ctx.enter_context(nc.semaphore(name))

        def sems(name, n=2):
            return [sem(f"{name}{i}") for i in range(n)]

        x_ln = two("x_ln", [P, TB, D])
        x_res = two("x_res", [P, TB, D])
        wqk = two("w_qk", [P, WQK])
        wv = two("w_v", [P, WV])
        wof = two("w_of", [P, WOF])
        QS = two("q_stack", [P, H, T], BF16)
        KS = two("k_stack", [P, H, T], BF16)
        Vp = two("v_padded", [P, TB, H, VOCT])
        xnT = two("xnT", [P, T])
        PT = sb("probsT", [P, 4, 4, T])
        st1 = sb("st1", [P, TB, 6])
        mv1 = sb("mv1", [P, TB, 2])
        rs1 = sb("rs1", [P, TB])
        xh1 = sb("xh1", [P, TB, D])
        st2 = sb("st2", [P, TB, 6])
        mv2 = sb("mv2", [P, TB, 2])
        rs2 = sb("rs2", [P, TB])
        xh2 = sb("xh2", [P, TB, D])
        nhalf = sb("nhalf", [P, TB])
        bqk_s = sb("bqk_s", [P, 1])
        qscale = sb("qscale", [P, 1])
        word = sb("words", [1, 17])
        qk32 = sb("qk32", [P, 2, T])
        qk_r = sb("qk_rest", [P, 2, T])
        parts = sb("parts", [P, 2, 3, T], BF16)
        zero2 = sb("zero2", [2, H * T // 2], BF16)
        nmax = sb("nmax", [P, H, TB])
        nm_p = two("nm_parts", [P, 4, H // 2, TB], BF16)
        nmT = two("nmT", [64, P], BF16)
        oraw = sb("oraw", [P, 2, T])
        rsum = sb("rsum", [P, TB, H])
        on = sb("on", [P, TB, H, HD])
        onT = sb("onT", [P, T])
        xb = sb("xb", [P, TB, D])
        x1 = sb("x1", [P, TB, D])
        x1b = sb("x1b", [P, TB, D])
        xnT2 = sb("xnT2", [P, T])
        hT = sb("hT", [P, 4, T])
        xo = two("xo", [P, TB, D])
        ident = sb("ident", [P, P])
        identb = sb("identb", [P, P], BF16)

        ST = [ctx.enter_context(nc.psum_tensor(f"scoresT{i}", [P, 2, T], F32)) for i in range(2)]
        PV = ctx.enter_context(nc.psum_tensor("pv", [P, T], F32))
        W = [ctx.enter_context(nc.psum_tensor(f"work{i}", [P, T], F32)) for i in range(BANKS)]

        const_in = sem("const_in")
        x_ln_in, x_res_in, wqk_in, wv_in, wof_in = (sems(n) for n in ("x_ln_in", "x_res_in", "wqk_in", "wv_in", "wof_in"))
        parts_out = sems("parts_out")
        stack_in = [sems("stack_in_a"), sems("stack_in_b")]
        max_in = [sems("max_in_a"), sems("max_in_b")]
        x_out = sems("x_out")
        names = ["score", "ln1T", "q", "k", "v", "oT0", "oT1", "onT", "proj", "ln2T", "mT0", "mT1"]
        names += [f"ffn{i}_{c}" for i in (1, 2) for c in range(4)]
        ready = {n: sem(n + "_ready") for n in names}
        read = {n: sem(n + "_read") for n in names}
        per_step = {n: 1 for n in names} | {"score": NSCORE}
        var1, xh1_done = sem("var1"), sem("xh1_done")
        var2, pow2, xh2_done = sem("var2"), sem("pow2"), sem("xh2_done")
        bias_scaled = sem("bias_scaled")
        high_done, rest1, mid_done, low_done = sem("high_done"), sem("rest1"), sem("mid_done"), sem("low_done")
        nm_done = sems("nm_parts_done")
        scoresT_ready, exp_done, masked, pv_done = sem("scoresT_ready"), sem("exp_done"), sem("masked"), sem("pv_done")
        oraw_done = sems("oraw_done")
        xb_done, x1b_done = sem("xb_done"), sem("x1b_done")
        vp_init = sem("vp_init")

        def at(k, u, off):
            return 2 * k + (u + off)

        def active(k, u, off):
            return not isinstance(k, int) or 0 <= 2 * k + u + off < NSTEP

        def need(eng, s, per, n, c):
            v = n * per + c if per != 1 else n + c
            if not isinstance(v, int) or v > 0:
                eng.wait_ge(s, v)

        def need2(eng, s, per, k, u, off, back=0):
            v = k + ((u + off) // 2 + 1 - back)
            v = v * per
            if not isinstance(v, int) or v > 0:
                eng.wait_ge(s, v)

        def bank_free(eng, k, u, w):
            it = 0
            i = w - BANKS
            while True:
                if i < 0:
                    i += len(WORK)
                    it -= 1
                name, off, t = WORK[i]
                if isinstance(k, int) and 2 * k + u + it + 2 < 0:
                    return
                if active(k, u, off + it):
                    need(eng, read[name], per_step[name], at(k, u, off + it), 1 if t is None else t + 1)
                    return
                i -= BANKS

        def run(eng, body):
            for it in range(-3, 2):
                body(it // 2, it % 2)
            last = (NSTEP - 3) // 2
            with eng.Fori(1, last) as k:
                body(k, 0)
                body(k, 1)
            for it in range(2 * last, NSTEP + 1):
                body(it // 2, it % 2)

        block = ctx.enter_context(nc.Block())

        @block.sync
        def _(sp):
            for p in range(2):
                sp.dma_start(QS[p][M_ROW:P, :, :], qc_d).then_inc(const_in, 16)
                sp.dma_start(KS[p][M_ROW:P, :, :], kc_d).then_inc(const_in, 16)
            sp.dma_start(ident[:, :], id_d).then_inc(const_in, 16)
            sp.dma_start(identb[:, :], idb_d).then_inc(const_in, 16)

            def refill(k, u, g):
                n, p, hs = at(k, u, 2), u % 2, slice(8 * g, 8 * g + 8)
                for qk, stack in ((0, QS[p]), (1, KS[p])):
                    for row, part, count in ((0, 0, 3), (24, 1 if qk else 0, 2), (40, 2 if qk else 0, 1)):
                        src = scr[p][qk, part:part + count].rearrange("c (d h) t -> (c d) h t", h=H)[:, hs, :]
                        sp.dma_start(stack[row:row + 8 * count, hs, :], src).then_inc(stack_in[g][p], 16)
                sp.dma_start(QS[p][M_ROW:M_ROW + 2, hs, :], zero2[:, :].rearrange("p (h t) -> p h t", t=T)).then_inc(stack_in[g][p], 16)

            def maxima(k, u, off, g):
                n, p = at(k, u, off), (u + off) % 2
                need(sp, read[f"mT{g}"], 1, n, 1)
                for c in range(2):
                    sp.dma_start(QS[p][M_ROW + c:M_ROW + c + 1, 8 * g:8 * g + 8, :].rearrange("c h (i q) -> c (h i) q", q=P),
                                 nmT[g][32 * c:32 * c + 32, :]).then_inc(max_in[g][p], 16)

            def body(k, u):
                if active(k, u, 3):
                    n, p = at(k, u, 3), (u + 3) % 2
                    need2(sp, x_out[(u - 2) % 2], 16, k, u, -2)
                    need(sp, xh1_done, 1, n, -1)
                    sp.dma_start(x_ln[p][:, :, :], xs[n].rearrange("p (b d) -> p b d", d=D)).then_inc(x_ln_in[p], 16)
                    need(sp, read["k"], 1, n, -1)
                    sp.dma_start(wqk[p][:, :], wqk_d[n // NB]).then_inc(wqk_in[p], 16)
                if active(k, u, 2):
                    n, p = at(k, u, 2), (u + 2) % 2
                    need(sp, read["v"], 1, n, -1)
                    sp.dma_start(wv[p][:, :], wv_d[n // NB]).then_inc(wv_in[p], 16)
                if active(k, u, 0):
                    n, p = at(k, u, 0), u % 2
                    need(sp, xb_done, 1, n, -1)
                    sp.dma_start(x_res[p][:, :, :], xs[n].rearrange("p (b d) -> p b d", d=D)).then_inc(x_res_in[p], 16)
                    need(sp, read["ffn2_3"], 1, n, -1)
                    need(sp, x1b_done, 1, n, -1)
                    sp.dma_start(wof[p][:, :], wof_d[n // NB]).then_inc(wof_in[p], 16)
                if active(k, u, 0):
                    maxima(k, u, 0, 1)
                if active(k, u, 2):
                    n, p = at(k, u, 2), u % 2
                    need(sp, low_done, 4, n, 4)
                    for g in range(2):
                        need2(sp, stack_in[g][p], 112, k, u, 2, back=1)
                    for qk in range(2):
                        sp.dma_start(scr[p][qk].rearrange("c p t -> p c t"), parts[:, qk, :, :]).then_inc(parts_out[p], 16)
                    need2(sp, parts_out[p], 32, k, u, 2)
                    if active(k, u, 0):
                        need(sp, scoresT_ready, 32, n, -64 + 16)
                    refill(k, u, 0)
                if active(k, u, 1):
                    maxima(k, u, 1, 0)
                if active(k, u, -1):
                    n, p = at(k, u, -1), (u - 1) % 2
                    need(sp, read["ffn2_3"], 1, n, 1)
                    sp.dma_start(xs[n + NB].rearrange("p (b d) -> p b d", d=D), xo[p][:, :, :]).then_inc(x_out[p], 16)
                if active(k, u, 2):
                    n = at(k, u, 2)
                    if active(k, u, 0):
                        need(sp, scoresT_ready, 32, n, -64 + 32)
                    refill(k, u, 1)

            run(sp, body)
            for p in range(2):
                sp.wait_ge(x_out[p], 16 * (NSTEP // 2))

        @block.tensor
        def _(pe):
            pe.wait_ge(const_in, 16 * 6)
            pe.wait_ge(vp_init, 2)

            def scores_for_exp(k, u, s, v):
                r, j = s // 4, s % 4
                p = u % 2
                if s in (0, 8) and v == 0:
                    need2(pe, max_in[s // 8][p], 32, k, u, 0)
                need(pe, exp_done, 32, at(k, u, 0), 2 * s + v + 1 - 2)
                for a in range(2):
                    h = 4 * r + 2 * v + a
                    for rows, q0, q1 in ((KSTEP, j * P, (j + 1) * P), (KROW, (j + 1) * P, T)):
                        if q1 > q0:
                            last = nc.tensor.matmul(ST[v][:, a, q0 - j * P:q1 - j * P], KS[p][0:rows, h, j * P:(j + 1) * P],
                                                    QS[p][0:rows, h, q0:q1], start=True, stop=True)
                last.then_inc(scoresT_ready, 1)

            def weighted_values(k, u, off, s):
                r, j = s // 4, s % 4
                p = (u + off) % 2
                n = at(k, u, off)
                need(pe, masked, 16, n, s + 1)
                if s == 0:
                    need(pe, oraw_done[1], 1, n, 0)
                    need(pe, read["v"], 1, n, 1)
                if s == 12:
                    need(pe, oraw_done[0], 1, n, 1)
                for a in range(4):
                    last = nc.tensor.matmul(PV[32 * a:32 * a + 32, j * P:T], Vp[p][:, j, 4 * r + a, :],
                                            PT[:, j, a, 0:T - j * P], start=(s in (0, 12)), stop=(s in (11, 15)))
                last.then_inc(pv_done, 1)

            def work(k, u, w):
                name, off, t = WORK[w]
                n, p, out = at(k, u, off), (u + off) % 2, W[w % BANKS]
                bank_free(pe, k, u, w)
                if name == "score":
                    quad, (i, heads) = t // len(SCORE_TILES), SCORE_TILES[t % len(SCORE_TILES)]
                    if t == 0:
                        need2(pe, stack_in[0][p], 112, k, u, off)
                    if t == 2 * len(SCORE_TILES):
                        need2(pe, stack_in[1][p], 112, k, u, off)
                    width = (i + 1) * P
                    for m, a in enumerate(heads):
                        h = 4 * quad + a
                        for rows, k0, k1 in ((KROW, 0, i * P), (P, i * P, width)):
                            if k1 > k0:
                                last = nc.tensor.matmul(out[:, m * width + k0:m * width + k1], QS[p][0:rows, h, i * P:(i + 1) * P],
                                                        KS[p][0:rows, h, k0:k1], start=True, stop=True)
                elif name == "ln1T":
                    need(pe, xh1_done, 1, n, 1)
                    for b in range(TB):
                        last = nc.tensor.transpose(out[:, b * P:(b + 1) * P], xh1[:, b, :], ident[:, :])
                elif name in ("q", "k"):
                    need(pe, read["ln1T"], 1, n, 1)
                    need2(pe, wqk_in[p], 16, k, u, off)
                    c = D * (name == "k")
                    last = nc.tensor.matmul(out[:, :], wqk[p][:, c:c + D], xnT[p][:, :], start=True, stop=True)
                elif name == "v":
                    need2(pe, wv_in[p], 16, k, u, off)
                    for b in range(TB):
                        last = nc.tensor.matmul(out[:, b * P:(b + 1) * P], xnT[p][:, b * P:(b + 1) * P], wv[p][:, 0:D],
                                                start=True, stop=True)
                elif name in ("oT0", "oT1"):
                    c = int(name[-1])
                    need(pe, oraw_done[c], 1, n, 1)
                    for b in range(TB):
                        last = nc.tensor.transpose(out[:, b * P:(b + 1) * P], oraw[:, c, b * P:(b + 1) * P], ident[:, :])
                elif name == "onT":
                    need(pe, read["oT1"], 1, n, 1)
                    for b in range(TB):
                        last = nc.tensor.transpose(out[:, b * P:(b + 1) * P], on[:, b, :, :].rearrange("p h d -> p (h d)"), ident[:, :])
                elif name == "proj":
                    need(pe, read["onT"], 1, n, 1)
                    need2(pe, wof_in[p], 16, k, u, off)
                    for b in range(TB):
                        last = nc.tensor.matmul(out[:, b * P:(b + 1) * P], onT[:, b * P:(b + 1) * P], wof[p][:, 0:D], start=True, stop=True)
                elif name == "ln2T":
                    need(pe, xh2_done, 1, n, 1)
                    for b in range(TB):
                        last = nc.tensor.transpose(out[:, b * P:(b + 1) * P], xh2[:, b, :], ident[:, :])
                elif name[:5] == "ffn1_":
                    c = int(name[-1])
                    need(pe, read["ln2T"], 1, n, 1)
                    last = nc.tensor.matmul(out[:, :], wof[p][:, (2 + c) * D:(3 + c) * D], xnT2[:, :], start=True, stop=True)
                elif name[:5] == "ffn2_":
                    b = int(name[-1])
                    need(pe, read["ffn1_3"], 1, n, 1)
                    for c in range(4):
                        last = nc.tensor.matmul(out[:, 0:P], hT[:, c, b * P:(b + 1) * P],
                                                wof[p][:, (6 + c) * D:(7 + c) * D], start=(c == 0), stop=(c == 3))
                else:
                    g = int(name[-1])
                    need(pe, nm_done[g], 1, n, 1)
                    last = nc.tensor.transpose(out[:, :].bitcast(BF16)[:, 0:P], nm_p[g][:, :, :, :].rearrange("p c h i -> p (c h i)"), identb[:, :])
                last.then_inc(ready[name], 1)

            def body(k, u):
                w = 0
                for s in range(16):
                    for piece, count in enumerate(pieces(s)):
                        if piece < 2 and active(k, u, 0):
                            scores_for_exp(k, u, s, piece)
                        off, back = (0, s - 2) if s >= 2 else (-1, s + 14)
                        if piece == 2 and active(k, u, off):
                            weighted_values(k, u, off, back)
                        for _ in range(count):
                            if active(k, u, WORK[w][1]):
                                work(k, u, w)
                            w += 1

            run(pe, body)

        @block.scalar
        def _(act):
            def exps(k, u, s, v):
                r, j = s // 4, s % 4
                width = T - j * P
                n = at(k, u, 0)
                need(act, pv_done, 16, n, s + 1 - 4)
                need(act, scoresT_ready, 32, n, 2 * s + v + 1)
                nc.scalar.activation(PT[:, j, 2 * v:2 * v + 2, 0:width], ST[v][:, :, 0:width], ACT.Exp).then_inc(exp_done, 1)

            def copy_sums(k, u, off, c):
                n = at(k, u, off)
                need(act, pv_done, 16, n, 16 if c else 12)
                need(act, ready[f"oT{c}"], 1, n, 0)
                nc.scalar.activation(oraw[:, c, :], PV[:, :], ACT.Copy).then_inc(oraw_done[c], 1)

            def work(k, u, w):
                name, off, t = WORK[w]
                n, p, src = at(k, u, off), (u + off) % 2, W[w % BANKS]
                if name == "ln1T":
                    need(act, ready["ln1T"], 1, n, 1)
                    need2(act, wqk_in[p], 16, k, u, off)
                    need(act, read["v"], 1, n, -1)
                    nc.scalar.activation(xnT[p][:, :], src[:, :], ACT.Identity, bias=wqk[p][:, 2 * D + 1:2 * D + 2],
                                         scale=wqk[p][:, 2 * D:2 * D + 1]).then_inc(read["ln1T"], 1)
                elif name in ("q", "k"):
                    i = int(name == "k")
                    need(act, ready[name], 1, n, 1)
                    bias, scale = (wqk[p][:, 2 * D + 3:2 * D + 4], 1.0) if i else (bqk_s[:, 0:1], 1.0 / math.sqrt(HD))
                    if not i:
                        need(act, bias_scaled, 1, n, 1)
                    need(act, rest1, 2, n, i - 1)
                    nc.scalar.activation(qk32[:, i, :], src[:, :], ACT.Identity, bias=bias, scale=scale).then_inc(read[name], 1)
                elif name == "onT":
                    need(act, ready["onT"], 1, n, 1)
                    need(act, ready["proj"], 1, n, 0)
                    nc.scalar.activation(onT[:, :], src[:, :], ACT.Copy).then_inc(read["onT"], 1)
                elif name == "ln2T":
                    need(act, ready["ln2T"], 1, n, 1)
                    need(act, ready["ffn1_3"], 1, n, 0)
                    nc.scalar.activation(xnT2[:, :], src[:, :], ACT.Identity, bias=wof[p][:, 11 * D + 1:11 * D + 2],
                                         scale=wof[p][:, 11 * D:11 * D + 1]).then_inc(read["ln2T"], 1)
                elif name[:5] == "ffn1_":
                    c = int(name[-1])
                    need(act, ready[name], 1, n, 1)
                    if c == 0:
                        need(act, ready["ffn2_3"], 1, n, 0)
                    nc.scalar.activation(hT[:, c, :], src[:, :], ACT.Gelu,
                                         bias=wof[p][:, 11 * D + 2 + c:11 * D + 3 + c]).then_inc(read[name], 1)

            def high_parts(k, u, i):
                n, p = at(k, u, 2), u % 2
                need(act, read["k" if i else "q"], 1, n, 1)
                need2(act, parts_out[(p + 1) % 2], 32, k, u, 1)
                nc.scalar.activation(parts[:, i, 2 * i, :], qk32[:, i, :], ACT.Copy).then_inc(high_done, 1)

            def middle_parts(k, u, i):
                n = at(k, u, 2)
                need(act, rest1, 2, n, i + 1)
                nc.scalar.activation(parts[:, i, 1, :], qk_r[:, i, :], ACT.Copy).then_inc(mid_done, 1)

            def body(k, u):
                w = 0
                for s in range(16):
                    if s == 2 and active(k, u, -1):
                        copy_sums(k, u, -1, 1)
                    if s == 14 and active(k, u, 0):
                        copy_sums(k, u, 0, 0)
                    for piece, count in enumerate(pieces(s)):
                        if piece < 2 and active(k, u, 0):
                            exps(k, u, s, piece)
                        for _ in range(count):
                            if active(k, u, WORK[w][1]):
                                work(k, u, w)
                            w += 1
                    if active(k, u, 2):
                        if s in (7, 9):
                            high_parts(k, u, s // 9)
                        if s in (8, 10):
                            middle_parts(k, u, s // 10)

            run(act, body)

        @block.vector
        def _(dve):
            nc.vector.memset(nhalf[:, :], -0.5)
            nc.vector.memset(qscale[:, :], 1.0 / math.sqrt(HD))
            nc.vector.memset(zero2[:, :], 0.0)
            for p in range(2):
                nc.vector.memset(nm_p[p][:, :, :, :], 0.0)
                nc.vector.memset(Vp[p][:, :, :, :].rearrange("p b h c -> p (b h c)"), 0.0)
            dve.drain()
            for p in range(2):
                for r in range(QUADS):
                    c = 24 + r % 3
                    last = nc.vector.memset(Vp[p][:, :, 4 * r:4 * r + 4, c:c + 1], 1.0)
                last.then_inc(vp_init, 1)

            def stats(src, st, mv, done):
                for b in range(TB):
                    nc.vector.bn_stats(st[:, b, :], src[:, b, :])
                dve.drain()
                for b in range(TB):
                    nc.vector.bn_aggr(mv[:, b, :], st[:, b, :])
                dve.drain()
                nc.vector.tensor_scalar(mv[:, :, 1], mv[:, :, 1], EPS, None, ALU.add).then_inc(done, 1)

            def standardise(src, mv, rs, dst, done):
                for b in range(TB):
                    last = nc.vector.tensor_scalar(dst[:, b, :], src[:, b, :], mv[:, b, 0:1], rs[:, b:b + 1], ALU.subtract, ALU.mult)
                last.then_inc(done, 1)

            def work(k, u, w):
                name, off, t = WORK[w]
                n, p, src = at(k, u, off), (u + off) % 2, W[w % BANKS]
                if name == "score":
                    quad, (i, heads) = t // len(SCORE_TILES), SCORE_TILES[t % len(SCORE_TILES)]
                    h = 4 * quad + heads[0]
                    need(dve, ready["score"], NSCORE, n, t + 1)
                    nc.vector.tensor_reduce(nmax[:, h:h + len(heads), i], src[:, 0:len(heads) * (i + 1) * P].rearrange(
                        "p (h c) -> p h c", h=len(heads)), AX.X, ALU.max, negate=True).then_inc(read["score"], 1)
                elif name == "v":
                    need(dve, ready["v"], 1, n, 1)
                    need2(dve, wv_in[p], 16, k, u, off)
                    need(dve, pv_done, 16, n, -16)
                    for r in range(QUADS):
                        c = 8 * (r % 3)
                        bv = wv[p][:, D + 32 * r:D + 32 * r + 32].rearrange("p (a d) -> p a d", d=HD)
                        last = nc.vector.tensor_tensor(
                            Vp[p][:, :, 4 * r:4 * r + 4, c:c + HD],
                            src[:, :].rearrange("p (b h d) -> p b h d", b=TB, d=HD)[:, :, 4 * r:4 * r + 4, :],
                            bv.unsqueeze(1).to_broadcast([P, TB, 4, HD]), ALU.add)
                    last.then_inc(read["v"], 1)
                elif name in ("oT0", "oT1"):
                    c = int(name[-1])
                    need(dve, ready[name], 1, n, 1)
                    if c == 0:
                        need(dve, ready["onT"], 1, n, 0)
                    tile = src[:, :].rearrange("p (b a c) -> p b a c", b=TB, a=4)
                    rs = range(3) if c == 0 else (3,)
                    for r in rs:
                        nc.vector.reciprocal(rsum[:, :, 4 * r:4 * r + 4], tile[:, :, :, 24 + r % 3])
                    dve.drain()
                    for r in rs:
                        last = nc.vector.tensor_tensor(on[:, :, 4 * r:4 * r + 4, :], tile[:, :, :, 8 * (r % 3):8 * (r % 3) + 8],
                                                       rsum[:, :, 4 * r:4 * r + 4].unsqueeze(3).to_broadcast([P, TB, 4, HD]), ALU.mult)
                    last.then_inc(read[name], 1)
                elif name == "proj":
                    need(dve, ready["proj"], 1, n, 1)
                    need(dve, xb_done, 1, n, 1)
                    need(dve, x1b_done, 1, n, 0)
                    nc.vector.tensor_tensor(x1[:, :, :], src[:, :].rearrange("p (b d) -> p b d", b=TB), xb[:, :, :], ALU.add).then_inc(read["proj"], 1)
                    dve.drain()
                    stats(x1, st2, mv2, var2)
                elif name[:5] == "ffn2_":
                    b = int(name[-1])
                    need(dve, ready[name], 1, n, 1)
                    if b == 0:
                        need(dve, x1b_done, 1, n, 1)
                        need2(dve, x_out[p], 16, k, u, off, back=1)
                    nc.vector.tensor_tensor(xo[p][:, b, :], src[:, 0:P], x1b[:, b, :], ALU.add).then_inc(read[name], 1)
                elif name in ("mT0", "mT1"):
                    g = int(name[-1])
                    need(dve, ready[name], 1, n, 1)
                    need2(dve, max_in[g][(p + 1) % 2], 32, k, u, off - 1)
                    nc.vector.tensor_copy(nmT[g][:, :], src[:, :].bitcast(BF16)[0:64, 0:P]).then_inc(read[name], 1)

            def body(k, u):
                w = 0
                for s in range(16):
                    if s == 12 and active(k, u, 3):
                        p = (u + 3) % 2
                        need2(dve, x_ln_in[p], 16, k, u, 3)
                        need(dve, xh1_done, 1, at(k, u, 3), 0)
                        stats(x_ln[p], st1, mv1, var1)
                    if s == 10 and active(k, u, -1):
                        n = at(k, u, -1)
                        need(dve, pow2, 1, n, 1)
                        need(dve, ready["ln2T"], 1, n, 0)
                        standardise(x1, mv2, rs2, xh2, xh2_done)
                    for _ in range(len(SCORES[s]) + len(MISC.get(s, []))):
                        if active(k, u, WORK[w][1]):
                            work(k, u, w)
                        w += 1
                    if s in (8, 15) and active(k, u, 1):
                        n, g = at(k, u, 1), s // 15
                        dve.drain()
                        need(dve, ready[f"mT{g}"], 1, n, 0)
                        nc.vector.tensor_copy(nm_p[g][:, 0, :, :], nmax[:, 8 * g:8 * g + 8, :])
                        dve.drain()
                        nc.vector.tensor_tensor(nm_p[g][:, 1, :, :], nmax[:, 8 * g:8 * g + 8, :], nm_p[g][:, 0, :, :],
                                                ALU.subtract).then_inc(nm_done[g], 1)

            run(dve, body)

        @block.gpsimd
        def _(pool):
            nc.gpsimd.memset(word[:, :], 0.0)

            def rest(k, u, i):
                n = at(k, u, 2)
                need(pool, high_done, 2, n, i + 1)
                nc.gpsimd.tensor_tensor(qk_r[:, i, :], qk32[:, i, :], parts[:, i, 2 * i, :], ALU.subtract).then_inc(rest1, 1)

            def low(k, u, i):
                n = at(k, u, 2)
                need(pool, mid_done, 2, n, i + 1)
                nc.gpsimd.tensor_tensor(parts[:, i, 2 - 2 * i, :], qk_r[:, i, :], parts[:, i, 1, :], ALU.subtract).then_inc(low_done, 2)

            def body(k, u):
                for s in range(16):
                    if active(k, u, 0):
                        n, j = at(k, u, 0), s % 4
                        need(pool, exp_done, 32, n, 2 * s + 2)
                        nc.gpsimd.tensor_tensor(word[:, 1 + s:2 + s], word[:, 0:1], word[:, 0:1], ALU.add)
                        blk = PT[:, j, :, 0:P]
                        nc.gpsimd.affine_select(out=blk, in_=blk, pattern=[[0, 4], [1, P]], compare_op=ALU.is_ge, fill=0.0,
                                                base=0, channel_multiplier=-1).then_inc(masked, 1)
                    if s == 0 and active(k, u, 2):
                        n, p = at(k, u, 2), u % 2
                        need(pool, var1, 1, n, 1)
                        need(pool, ready["ln1T"], 1, n, 0)
                        nc.gpsimd.tensor_tensor(rs1[:, :], mv1[:, :, 1], nhalf[:, :], ALU.pow)
                        pool.drain()
                        need2(pool, wqk_in[p], 16, k, u, 2)
                        need(pool, read["q"], 1, n, 0)
                        nc.gpsimd.tensor_tensor(bqk_s[:, :], wqk[p][:, 2 * D + 2:2 * D + 3], qscale[:, :], ALU.mult).then_inc(bias_scaled, 1)
                    if s < TB and active(k, u, 2):
                        last = nc.gpsimd.tensor_scalar(xh1[:, s, :], x_ln[u % 2][:, s, :], mv1[:, s, 0:1], rs1[:, s:s + 1], ALU.subtract, ALU.mult)
                        if s == TB - 1:
                            last.then_inc(xh1_done, 1)
                    if s == 4 and active(k, u, -1):
                        n, p = at(k, u, -1), (u - 1) % 2
                        need2(pool, x_res_in[p], 16, k, u, -1)
                        need2(pool, wof_in[p], 16, k, u, -1)
                        need(pool, read["proj"], 1, n, 0)
                        nc.gpsimd.tensor_tensor(xb[:, :, :], x_res[p][:, :, :], wof[p][:, D:2 * D].unsqueeze(1).to_broadcast([P, TB, D]),
                                                ALU.add).then_inc(xb_done, 1)
                    if s == 8 and active(k, u, -1):
                        n, p = at(k, u, -1), (u - 1) % 2
                        need(pool, var2, 1, n, 1)
                        need(pool, xh2_done, 1, n, 0)
                        nc.gpsimd.tensor_tensor(rs2[:, :], mv2[:, :, 1], nhalf[:, :], ALU.pow).then_inc(pow2, 1)
                        need(pool, read["ffn2_3"], 1, n, 0)
                        nc.gpsimd.tensor_tensor(x1b[:, :, :], x1[:, :, :], wof[p][:, 10 * D:11 * D].unsqueeze(1).to_broadcast([P, TB, D]),
                                                ALU.add).then_inc(x1b_done, 1)
                    if active(k, u, 2):
                        if s in (7, 9):
                            rest(k, u, s // 9)
                        if s in (8, 10):
                            low(k, u, s // 10)

            run(pool, body)


def modulation_program(nc, NB, T, io):
    TB = T // P
    NM = 6 * D
    DEPTH = 4
    GROUPS = NB // DEPTH
    with ExitStack() as ctx:
        def sb(name, shape, dt=F32):
            return ctx.enter_context(nc.sbuf_tensor(name, shape, dt))

        def sem(name):
            return ctx.enter_context(nc.semaphore(name))

        cT = sb("cT", [P, NB])
        scT = sb("scT", [P, NB])
        wmod = sb("wmod", [P, NM])
        mod = sb("mod", [NB, 6, D])
        gate_abs = sb("gate_abs", [NB, 2, D])
        gate_sign = sb("gate_sign", [NB, 2, D])
        x0 = [sb(f"x0_{i}", [P, TB, D]) for i in range(DEPTH)]
        rows = [sb(f"mod_rows{i}", [P, 2, D]) for i in range(DEPTH)]
        st = sb("st0", [P, TB, 6])
        mv = [sb(f"mv0_{i}", [P, TB, 2]) for i in range(DEPTH)]
        rs = [sb(f"rs0_{i}", [P, TB]) for i in range(DEPTH)]
        nh = sb("nhalf0", [P, TB])
        xh = sb("xh0", [P, TB, D])
        hm = [sb(f"hm0_{i}", [P, TB, D]) for i in range(DEPTH)]
        h = [sb(f"h0_{i}", [P, TB, D]) for i in range(DEPTH)]
        pm = ctx.enter_context(nc.psum_tensor("mod_ps", [NB, 2, 512], F32))
        c_in, silu_done, mod_ready, mod_done, mod_out = (sem(n) for n in ("c_in", "silu_done", "mod_ready", "mod_done", "mod_out"))
        x0_in = [sem(f"x0_in{i}") for i in range(DEPTH)]
        h_out = [sem(f"h_out{i}") for i in range(DEPTH)]
        var_done, pow_done, scaled, h_done = sem("var0"), sem("pow0"), sem("scaled0"), sem("h0_done")
        block = ctx.enter_context(nc.Block())

        @block.sync
        def _(sp):
            sp.dma_start(cT[:, :], io["cT"]).then_inc(c_in, 16)
            sp.dma_start(wmod[:, :], io["wmod"]).then_inc(c_in, 16)
            sp.wait_ge(mod_done, 1)
            sp.dma_start(io["mod"], mod[:, :, :].rearrange("b c d -> b (c d)")).then_inc(mod_out, 16)
            sp.wait_ge(mod_out, 16)

            def load(k, u, b):
                sp.dma_start(x0[u][:, :, :], io["x"][b].rearrange("(t p) d -> p t d", p=P)).then_inc(x0_in[u], 16)
                sp.dma_start(rows[u][:, :, :].rearrange("p c d -> p (c d)"), io["mod"][b, 0:2 * D].partition_broadcast(P)).then_inc(x0_in[u], 16)

            def store(k, u, b):
                sp.wait_ge(h_done, b + 1)
                sp.dma_start(io["xs"][b].rearrange("p (t d) -> p t d", d=D), h[u][:, :, :]).then_inc(h_out[u], 16)

            for u in range(DEPTH):
                load(0, u, u)
            with sp.Fori(0, GROUPS - 1) as k:
                for u in range(DEPTH):
                    store(k, u, DEPTH * k + u)
                    load(k, u, DEPTH * k + u + DEPTH)
            for u in range(DEPTH):
                store(GROUPS - 1, u, NB - DEPTH + u)
            for u in range(DEPTH):
                sp.wait_ge(h_out[u], 16 * GROUPS)

        @block.scalar
        def _(act):
            act.wait_ge(c_in, 32)
            nc.scalar.activation(scT[:, :], cT[:, :], ACT.Silu).then_inc(silu_done, 1)

        @block.tensor
        def _(pe):
            pe.wait_ge(silu_done, 1)
            for i in range(2):
                last = nc.tensor.matmul(pm[:, i, 0:NM // 2], scT[:, :], wmod[:, i * NM // 2:(i + 1) * NM // 2], start=True, stop=True)
            last.then_inc(mod_ready, 1)

        @block.vector
        def _(dve):
            dve.wait_ge(mod_ready, 1)
            for i in range(2):
                nc.vector.tensor_copy(mod[:, 3 * i:3 * i + 3, :].rearrange("b c d -> b (c d)"), pm[:, i, 0:NM // 2])
            nc.vector.memset(nh[:, :], -0.5)
            dve.drain()
            both = mod[:, :, :].rearrange("b (i c) d -> b i c d", c=3)
            nc.vector.tensor_scalar(gate_sign[:, :, :], both[:, :, 2, :], 0.0, 2.0, ALU.is_ge, ALU.mult)
            nc.vector.scalar_tensor_tensor(out=gate_abs[:, :, :], in0=both[:, :, 2, :], scalar=-1.0, in1=both[:, :, 2, :],
                                           op0=ALU.mult, op1=ALU.max)
            nc.vector.tensor_scalar(both[:, :, 1, :], both[:, :, 1, :], 1.0, None, ALU.add)
            dve.drain()
            nc.vector.tensor_scalar(gate_abs[:, :, :], gate_abs[:, :, :], 0.25, None, ALU.max)
            dve.drain()
            nc.vector.scalar_tensor_tensor(out=both[:, :, 2, :], in0=gate_sign[:, :, :], scalar=-1.0, in1=gate_abs[:, :, :],
                                           op0=ALU.add, op1=ALU.mult).then_inc(mod_done, 1)

            def statistics(k, u):
                dve.wait_ge(x0_in[u], 32 * k + 32)
                for t in range(TB):
                    nc.vector.bn_stats(st[:, t, :], x0[u][:, t, :])
                dve.drain()
                for t in range(TB):
                    nc.vector.bn_aggr(mv[u][:, t, :], st[:, t, :])
                dve.drain()
                nc.vector.tensor_scalar(mv[u][:, :, 1], mv[u][:, :, 1], EPS, None, ALU.add).then_inc(var_done, 1)

            def scaled_rows(k, u):
                b = DEPTH * k + u
                dve.wait_ge(pow_done, b + 1)
                for t in range(TB):
                    nc.vector.tensor_scalar(xh[:, t, :], x0[u][:, t, :], mv[u][:, t, 0:1], rs[u][:, t:t + 1], ALU.subtract, ALU.mult)
                dve.drain()
                if not isinstance(k, int) or k > 0:
                    dve.wait_ge(h_done, b - DEPTH + 1)
                nc.vector.tensor_tensor(hm[u][:, :, :], xh[:, :, :], rows[u][:, 1:2, :].to_broadcast([P, TB, D]), ALU.mult).then_inc(scaled, 1)
                dve.drain()

            def group(k, last):
                for u in range(DEPTH):
                    if u + 1 < DEPTH:
                        statistics(k, u + 1)
                    elif not last:
                        statistics(k + 1, 0)
                    scaled_rows(k, u)

            statistics(0, 0)
            group(0, False)
            with dve.Fori(1, GROUPS - 1) as k:
                group(k, False)
            group(GROUPS - 1, True)

        @block.gpsimd
        def _(pool):
            def inverse_root(k, u):
                pool.wait_ge(var_done, DEPTH * k + u + 1)
                nc.gpsimd.tensor_tensor(rs[u][:, :], mv[u][:, :, 1], nh[:, :], ALU.pow).then_inc(pow_done, 1)

            def shifted_rows(k, u):
                pool.wait_ge(scaled, DEPTH * k + u + 1)
                if not isinstance(k, int) or k > 0:
                    pool.wait_ge(h_out[u], 16 * k)
                nc.gpsimd.tensor_tensor(h[u][:, :, :], hm[u][:, :, :], rows[u][:, 0:1, :].to_broadcast([P, TB, D]), ALU.add).then_inc(h_done, 1)

            def group(k, last):
                for u in range(DEPTH):
                    if u + 1 < DEPTH:
                        inverse_root(k, u + 1)
                    elif not last:
                        inverse_root(k + 1, 0)
                    shifted_rows(k, u)

            inverse_root(0, 0)
            group(0, False)
            with pool.Fori(1, GROUPS - 1) as k:
                group(k, False)
            group(GROUPS - 1, True)


def experts_program(nc, NB, L, T, io):
    TB = T // P
    NM = 6 * D
    with ExitStack() as ctx:
        def sb(name, shape, dt=F32):
            return ctx.enter_context(nc.sbuf_tensor(name, shape, dt))

        def two(name, shape, dt=F32):
            return [sb(f"{name}{i}", shape, dt) for i in range(2)]

        def ps(name, shape):
            return ctx.enter_context(nc.psum_tensor(name, shape, F32))

        def sem(name):
            return ctx.enter_context(nc.semaphore(name))

        y = two("y_rows", [P, TB, D])
        x0 = two("x_rows", [P, TB, D])
        rows = two("mod_rows_e", [P, 3, D])
        gate_row = two("gate_row", [P, D])
        fin = sb("final_wb", [P, 2, D])
        gate_w = sb("gate_w", [P, E])
        w1 = sb("w1_e", [P, E, EH * P])
        b1 = sb("b1_e", [P, E * EH])
        w2 = sb("w2_e", [P, E, EH, D])
        b2 = sb("b2_e", [E, D])
        rank = sb("rank", [P, E])
        ident = sb("ident_e", [P, P])
        nh = sb("nhalf_e", [P, TB])
        st, mv, rs = sb("st_e", [P, TB, 6]), sb("mv_e", [P, TB, 2]), sb("rs_e", [P, TB])
        xh = sb("xh_e", [P, TB, D])
        g12 = sb("g12", [P, 2, D])
        xg = sb("x_plus_gfb", [P, TB, D])
        yg = sb("y_times_gfw", [P, TB, D])
        x1 = two("x1_e", [P, TB, D])
        h2a = sb("h2a", [P, TB, D])
        h2 = sb("h2", [P, TB, D])
        h2T = two("h2T", [P, T])
        lg, ex, pr, p2, eq, wr, oh1, oh2 = (sb(n, [P, TB, E]) for n in ("lg", "ex", "pr", "p2", "eq", "wr", "oh1", "oh2"))
        mx, sm, rc = (sb(n, [P, TB]) for n in ("mx", "sm", "rc"))
        gt = two("gates", [P, TB, E])
        gT = two("gatesT", [E, T])
        hs = two("hidden", [P, EH, T])
        acc = sb("acc", [P, TB, D])
        accg = sb("acc_gated", [P, TB, D])
        out = two("out_rows", [P, TB, D])
        hp = [ps(f"hidden_ps{i}", [P, EH, T]) for i in range(2)]
        op = [ps(f"expert_ps{i}", [P, TB, D]) for i in range(2)]
        tp = ps("transposed_ps", [P, T])
        gp = ps("router_ps", [P, T])

        w_in = sem("w_in")
        gate_in = [sem(f"gate_in{i}") for i in range(2)]
        y_in, out_out = [sem(f"y_in{i}") for i in range(2)], [sem(f"out_out{i}") for i in range(2)]
        (init_done, var_done, pow_done, g12_done, xg_done, x1_done, h2_done, h2T_ready, h2T_done, lg_ready, lg_done, ex_done,
         gates_done, gT_ready, gT_done, b2_ready, b2_read, hid_ready, hid_done, exp_ready, exp_read, out_done) = (
            sem("e_" + n) for n in ("init_done", "var_done", "pow_done", "g12_done", "xg_done", "x1_done", "h2_done", "h2T_ready",
                                    "h2T_done", "lg_ready", "lg_done", "ex_done", "gates_done", "gT_ready", "gT_done", "b2_ready",
                                    "b2_read", "hid_ready", "hid_done", "exp_ready", "exp_read", "out_done"))

        def need(eng, s, v):
            if not isinstance(v, int) or v > 0:
                eng.wait_ge(s, v)

        def run(eng, first, pair):
            first()
            for u in range(2):
                pair(0, u, True)
            with eng.Fori(1, NB // 2 - 1) as k:
                for u in range(2):
                    pair(k, u, True)
            for u in range(2):
                pair(NB // 2 - 1, u, u == 0)

        block = ctx.enter_context(nc.Block())

        @block.sync
        def _(sp):
            for dst, src in ((fin[:, :, :].rearrange("p c d -> p (c d)"), io["final"].partition_broadcast(P)), (gate_w[:, :], io["gate"]),
                             (rank[:, :], io["rank"].partition_broadcast(P)), (ident[:, :], io["ident"]), (b1[:, :], io["b1"]), (b2[:, :], io["b2"]),
                             (w1[:, :, :], io["w1"].rearrange("e d h -> d e h")),
                             (w2[:, :, :, :].rearrange("p e c d -> p (e c) d"), io["w2"].rearrange("e (c p) d -> p (e c) d", p=P))):
                sp.dma_start(dst, src).then_inc(w_in, 16)

            def load(b, u):
                sp.dma_start(y[u][:, :, :], io["xs"][L * NB + b].rearrange("p (t d) -> p t d", d=D)).then_inc(y_in[u], 16)
                sp.dma_start(x0[u][:, :, :], io["x"][b].rearrange("(t p) d -> p t d", p=P)).then_inc(y_in[u], 16)
                sp.dma_start(rows[u][:, :, :].rearrange("p c d -> p (c d)"), io["mod"][b, 2 * D:5 * D].partition_broadcast(P)).then_inc(y_in[u], 16)

            def load_gate(b, u):
                sp.dma_start(gate_row[u][:, :], io["mod"][b, 5 * D:6 * D].partition_broadcast(P)).then_inc(gate_in[u], 16)

            def pair(k, u, more):
                b = 2 * k + u
                if not isinstance(k, int) or b + 2 < NB:
                    sp.wait_ge(h2_done, b + 1)
                    load(b + 2, u)
                sp.wait_ge(out_done, b + 1)
                sp.dma_start(io["out"][b].rearrange("(t p) d -> p t d", p=P), out[u][:, :, :]).then_inc(out_out[u], 16)
                if not isinstance(k, int) or b + 2 < NB:
                    load_gate(b + 2, u)

            def first():
                load(0, 0)
                load(1, 1)
                load_gate(0, 0)
                load_gate(1, 1)

            run(sp, first, pair)
            for u in range(2):
                sp.wait_ge(out_out[u], 16 * (NB // 2))

        @block.tensor
        def _(pe):
            def up(b, u, e):
                need(pe, hid_done, 2 * (8 * b + e + 1) - 4)
                if e == 0:
                    pe.wait_ge(h2T_done, b + 1)
                for c in range(EH):
                    last = nc.tensor.matmul(hp[e % 2][:, c, :], w1[:, e, c * P:(c + 1) * P], h2T[u][:, :], start=True, stop=True)
                last.then_inc(hid_ready, 1)

            def down(b, e):
                pe.wait_ge(hid_done, 2 * (8 * b + e + 1))
                need(pe, exp_read, 8 * b + e - 1)
                for t in range(TB):
                    for c in range(EH):
                        last = nc.tensor.matmul(op[e % 2][:, t, :], hs[e % 2][:, c, t * P:(t + 1) * P], w2[:, e, c, :],
                                                start=(c == 0), stop=(c == EH - 1))
                last.then_inc(exp_ready, 1)

            def transposes(b):
                pe.wait_ge(h2_done, b + 1)
                need(pe, h2T_done, b)
                for t in range(TB):
                    last = nc.tensor.transpose(tp[:, t * P:(t + 1) * P], h2[:, t, :], ident[:, :])
                last.then_inc(h2T_ready, 1)

            def router(b, u):
                pe.wait_ge(h2T_done, b + 1)
                need(pe, b2_read, b)
                for t in range(TB):
                    last = nc.tensor.matmul(gp[:, t * E:(t + 1) * E], h2T[u][:, t * P:(t + 1) * P], gate_w[:, :], start=True, stop=True)
                last.then_inc(lg_ready, 1)

            def gates_transposed(b, u):
                pe.wait_ge(gates_done, b + 1)
                for t in range(TB):
                    last = nc.tensor.transpose(gp[0:E, t * P:(t + 1) * P], gt[u][:, t, :], ident[:, :])
                last.then_inc(gT_ready, 1)

            def biases(b, u):
                pe.wait_ge(gT_done, b + 1)
                for t in range(TB):
                    last = nc.tensor.matmul(gp[:, t * P:(t + 1) * P], gT[u][:, t * P:(t + 1) * P], b2[:, :], start=True, stop=True)
                last.then_inc(b2_ready, 1)

            def first():
                pe.wait_ge(w_in, 16 * 8)
                transposes(0)
                router(0, 0)

            def pair(k, u, more):
                b = 2 * k + u
                up(b, u, 0)
                for e in range(E):
                    if e + 1 < E:
                        up(b, u, e + 1)
                    down(b, e)
                    if e == 1:
                        gates_transposed(b, u)
                    if e == 2:
                        biases(b, u)
                    if more and e == 4:
                        transposes(b + 1)
                    if more and e == 5:
                        router(b + 1, 1 - u)

            run(pe, first, pair)

        @block.scalar
        def _(act):
            def transposed(b, u):
                act.wait_ge(h2T_ready, b + 1)
                need(act, hid_ready, 8 * b - 8)
                nc.scalar.activation(h2T[u][:, :], tp[:, :], ACT.Copy).then_inc(h2T_done, 1)

            def router(b, u):
                act.wait_ge(lg_done, b + 1)
                nc.scalar.activation(ex[:, :, :], lg[:, :, :], ACT.Exp).then_inc(ex_done, 1)

            def gates(b, u):
                act.wait_ge(gT_ready, b + 1)
                need(act, b2_ready, b - 1)
                nc.scalar.activation(gT[u][:, :], gp[0:E, :], ACT.Copy).then_inc(gT_done, 1)

            def first():
                act.wait_ge(w_in, 16 * 8)
                transposed(0, 0)
                router(0, 0)

            def pair(k, u, more):
                b = 2 * k + u
                for e in range(E):
                    act.wait_ge(hid_ready, 8 * b + e + 1)
                    need(act, exp_ready, 8 * b + e - 1)
                    for c in range(EH):
                        nc.scalar.activation(hs[e % 2][:, c, :], hp[e % 2][:, c, :], ACT.Relu,
                                             bias=b1[:, e * EH + c:e * EH + c + 1]).then_inc(hid_done, 1)
                    if e == 1:
                        gates(b, u)
                    if more and e == 4:
                        transposed(b + 1, 1 - u)
                    if more and e == 6:
                        router(b + 1, 1 - u)

            run(act, first, pair)

        @block.vector
        def _(dve):
            def stats(src):
                for t in range(TB):
                    nc.vector.bn_stats(st[:, t, :], src[:, t, :])
                dve.drain()
                for t in range(TB):
                    nc.vector.bn_aggr(mv[:, t, :], st[:, t, :])
                dve.drain()
                nc.vector.tensor_scalar(mv[:, :, 1], mv[:, :, 1], EPS, None, ALU.add).then_inc(var_done, 1)

            def standardise(src):
                for t in range(TB):
                    nc.vector.tensor_scalar(xh[:, t, :], src[:, t, :], mv[:, t, 0:1], rs[:, t:t + 1], ALU.subtract, ALU.mult)
                dve.drain()

            def by_row(u, c):
                return rows[u][:, c:c + 1, :].to_broadcast([P, TB, D])

            def over(v):
                return v[:, :].unsqueeze(2).to_broadcast([P, TB, E])

            def pre1(k, b, u, half):
                dve.wait_ge(y_in[u], 48 * half)
                stats(y[u])
                need(dve, xg_done, b)
                nc.vector.tensor_tensor(g12[:, :, :], fin[:, :, :], rows[u][:, 0:1, :].to_broadcast([P, 2, D]), ALU.mult).then_inc(g12_done, 1)

            def pre2(k, b, u):
                dve.wait_ge(pow_done, 2 * b + 1)
                standardise(y[u])
                nc.vector.tensor_tensor(yg[:, :, :], xh[:, :, :], g12[:, 0:1, :].to_broadcast([P, TB, D]), ALU.mult)
                dve.drain()
                dve.wait_ge(xg_done, b + 1)
                nc.vector.tensor_tensor(x1[u][:, :, :], yg[:, :, :], xg[:, :, :], ALU.add).then_inc(x1_done, 1)
                dve.drain()
                stats(x1[u])

            def pre3(k, b, u):
                dve.wait_ge(pow_done, 2 * b + 2)
                standardise(x1[u])
                nc.vector.tensor_tensor(h2a[:, :, :], xh[:, :, :], by_row(u, 2), ALU.mult)
                dve.drain()
                need(dve, h2T_ready, b)
                nc.vector.tensor_tensor(h2[:, :, :], h2a[:, :, :], by_row(u, 1), ALU.add).then_inc(h2_done, 1)

            def route1(b, u):
                dve.wait_ge(lg_ready, b + 1)
                z = gp[:, 0:TB * E].rearrange("p (t e) -> p t e", e=E)
                nc.vector.tensor_reduce(mx[:, :], z, AX.X, ALU.max)
                dve.drain()
                nc.vector.tensor_tensor(lg[:, :, :], z, over(mx), ALU.subtract).then_inc(lg_done, 1)

            def largest(src, dst):
                nc.vector.tensor_reduce(mx[:, :], src[:, :, :], AX.X, ALU.max)
                dve.drain()
                nc.vector.tensor_tensor(eq[:, :, :], src[:, :, :], over(mx), ALU.is_equal)
                dve.drain()
                nc.vector.tensor_tensor(wr[:, :, :], eq[:, :, :], rank[:, :].unsqueeze(1).to_broadcast([P, TB, E]), ALU.mult)
                dve.drain()
                nc.vector.tensor_reduce(sm[:, :], wr[:, :, :], AX.X, ALU.max)
                dve.drain()
                nc.vector.tensor_tensor(dst[:, :, :], wr[:, :, :], over(sm), ALU.is_equal)
                dve.drain()

            def route2(b, u):
                dve.wait_ge(ex_done, b + 1)
                nc.vector.tensor_reduce(sm[:, :], ex[:, :, :], AX.X, ALU.add)
                dve.drain()
                nc.vector.reciprocal(rc[:, :], sm[:, :])
                dve.drain()
                nc.vector.tensor_tensor(pr[:, :, :], ex[:, :, :], over(rc), ALU.mult)
                dve.drain()
                largest(pr, oh1)

            def route3(b, u):
                nc.vector.scalar_tensor_tensor(out=p2[:, :, :], in0=oh1[:, :, :], scalar=-4.0, in1=pr[:, :, :], op0=ALU.mult, op1=ALU.add)
                dve.drain()
                largest(p2, oh2)
                nc.vector.tensor_tensor(eq[:, :, :], oh1[:, :, :], oh2[:, :, :], ALU.add)
                dve.drain()
                nc.vector.tensor_tensor(wr[:, :, :], eq[:, :, :], pr[:, :, :], ALU.mult)
                dve.drain()
                nc.vector.tensor_reduce(sm[:, :], wr[:, :, :], AX.X, ALU.add)
                dve.drain()
                nc.vector.tensor_scalar(sm[:, :], sm[:, :], 1e-12, None, ALU.max)
                dve.drain()
                nc.vector.reciprocal(rc[:, :], sm[:, :])
                dve.drain()
                need(dve, gT_ready, b - 1)
                nc.vector.tensor_tensor(gt[u][:, :, :], wr[:, :, :], over(rc), ALU.mult).then_inc(gates_done, 1)
                dve.drain()

            def first():
                nc.vector.memset(nh[:, :], -0.5).then_inc(init_done, 1)
                dve.wait_ge(w_in, 16 * 8)
                pre1(0, 0, 0, 1)
                pre2(0, 0, 0)
                pre3(0, 0, 0)
                route1(0, 0)
                route2(0, 0)
                route3(0, 0)

            def pair(k, u, more):
                b = 2 * k + u
                for e in range(E):
                    dve.wait_ge(exp_ready, 8 * b + e + 1)
                    for t in range(TB):
                        gate = gt[u][:, t, e:e + 1]
                        if e == 0:
                            last = nc.vector.tensor_scalar(acc[:, t, :], op[e % 2][:, t, :], gate, None, ALU.mult)
                        else:
                            last = nc.vector.scalar_tensor_tensor(out=acc[:, t, :], in0=op[e % 2][:, t, :], scalar=gate,
                                                                  in1=acc[:, t, :], op0=ALU.mult, op1=ALU.add)
                    last.then_inc(exp_read, 1)
                    dve.drain()
                    if e == 3:
                        dve.wait_ge(b2_ready, b + 1)
                        nc.vector.tensor_tensor(acc[:, :, :].rearrange("p t d -> p (t d)"), gp[:, :],
                                                acc[:, :, :].rearrange("p t d -> p (t d)"), ALU.add).then_inc(b2_read, 1)
                        dve.drain()
                    if more and e == 0:
                        pre1(k, b + 1, 1 - u, k + u + 1)
                    if more and e == 1:
                        pre2(k, b + 1, 1 - u)
                    if more and e == 2:
                        pre3(k, b + 1, 1 - u)
                    if more and e == 5:
                        route1(b + 1, 1 - u)
                    if more and e == 6:
                        route2(b + 1, 1 - u)
                    if more and e == 7:
                        route3(b + 1, 1 - u)
                dve.wait_ge(gate_in[u], 16 * (k + 1))
                nc.vector.tensor_tensor(accg[:, :, :], acc[:, :, :], gate_row[u][:, :].unsqueeze(1).to_broadcast([P, TB, D]), ALU.mult)
                dve.drain()
                if not isinstance(k, int) or k > 0:
                    dve.wait_ge(out_out[u], 16 * k)
                nc.vector.tensor_tensor(out[u][:, :, :], accg[:, :, :], x1[u][:, :, :], ALU.add).then_inc(out_done, 1)

            run(dve, first, pair)

        @block.gpsimd
        def _(pool):
            def prepare(b, u, half):
                pool.wait_ge(var_done, 2 * b + 1)
                nc.gpsimd.tensor_tensor(rs[:, :], mv[:, :, 1], nh[:, :], ALU.pow).then_inc(pow_done, 1)
                pool.wait_ge(g12_done, b + 1)
                pool.wait_ge(y_in[u], 48 * half)
                need(pool, x1_done, b)
                nc.gpsimd.tensor_tensor(xg[:, :, :], x0[u][:, :, :], g12[:, 1:2, :].to_broadcast([P, TB, D]), ALU.add).then_inc(xg_done, 1)
                pool.wait_ge(var_done, 2 * b + 2)
                nc.gpsimd.tensor_tensor(rs[:, :], mv[:, :, 1], nh[:, :], ALU.pow).then_inc(pow_done, 1)

            def first():
                pool.wait_ge(init_done, 1)
                prepare(0, 0, 1)

            def pair(k, u, more):
                if more:
                    prepare(2 * k + u + 1, 1 - u, k + u + 1)

            run(pool, first, pair)



def tables(T):
    bf = mybir.dt.np(BF16)
    base = 2.0 ** (-(2.0 ** (-(math.log2(H) - 3))))
    slopes = (base ** np.arange(1, H + 1)).astype(np.float32).astype(np.float64)
    qc = np.zeros((P - M_ROW, H, T), np.float64)
    kc = np.zeros((P - M_ROW, H, T), np.float64)
    t = np.arange(T)
    tt = t % P
    kc[0:2] = 1.0
    rest = slopes[:, None] * (t - T // 2)[None]
    qc[2:5] = 1.0
    for i in range(3):
        part = rest.astype(bf).astype(np.float64)
        kc[2 + i] = part
        rest = rest - part
    for r in range(P // 8 - 1):
        kc[STEP_ROW - M_ROW + r] = tt >= 8 * (r + 1)
        qc[STEP_ROW - M_ROW + r] = np.where(tt < 8 * (r + 1), -2.0 ** 17, 0.0)
    for g in range(P // 8):
        kc[GROUP_ROW - M_ROW + g] = np.where(tt // 8 == g, 2.0 ** (18 * (tt % 8) - 2.0), 0.0)
        qc[GROUP_ROW - M_ROW + g] = np.where(tt // 8 == g, -(2.0 ** (-18.0 * (tt % 8))), 0.0)
    return qc.astype(bf), kc.astype(bf)


def kernel(**inputs):
    import concourse.bacc as _bacc
    from concourse.bass_utils import run_bass_kernel_spmd as _run

    a = {k: np.asarray(v) for k, v in inputs.items()}
    x = a["L0_attn_x"]
    NB, T, _ = x.shape
    L = a["L0_attn_in_proj_w"].shape[0]

    def dmajor(w):
        return w.reshape(L, H, HD, -1).transpose(0, 2, 1, 3).reshape(L, D, -1)

    def col(v):
        return v.reshape(L, D, 1)

    def row(v):
        return np.broadcast_to(v.reshape(L, 1, D), (L, P, D))

    w_in, b_in = a["L0_attn_in_proj_w"], a["L0_attn_in_proj_b"]
    f1 = a["L0_attn_ffn1_w"]
    tr = lambda w: w.transpose(0, 2, 1)
    wqk = np.concatenate([tr(dmajor(w_in[:, 0:D])), tr(dmajor(w_in[:, D:2 * D])), col(a["L0_attn_ln1_w"]), col(a["L0_attn_ln1_b"]),
                          dmajor(b_in[:, 0:D]), dmajor(b_in[:, D:2 * D])], axis=2)
    wv = np.concatenate([tr(w_in[:, 2 * D:]), row(b_in[:, 2 * D:])], axis=2)
    wof = np.concatenate([tr(a["L0_attn_out_proj_w"]), row(a["L0_attn_out_proj_b"]), tr(f1)]
                         + [tr(a["L0_attn_ffn2_w"])[:, c * P:(c + 1) * P] for c in range(4)]
                         + [row(a["L0_attn_ffn2_b"]), col(a["L0_attn_ln2_w"]), col(a["L0_attn_ln2_b"])]
                         + [a["L0_attn_ffn1_b"].reshape(L, 4, P).transpose(0, 2, 1)], axis=2)
    qc, kc = tables(T)
    arrays = {
        "x": x, "wqk": wqk, "wv": wv, "wof": wof, "qc": qc, "kc": kc,
        "ident": np.eye(P, dtype=np.float32), "identb": np.eye(P).astype(mybir.dt.np(BF16)),
        "cT": a["L0_c"].T, "wmod": a["L0_wmod"],
        "final": np.concatenate([a["L0_attn_final_w"], a["L0_attn_final_b"]]),
        "gate": a["L0_ffn_gate"], "w1": a["L0_ffn_W1"], "w2": a["L0_ffn_W2"], "b2": a["L0_ffn_b2"],
        "b1": a["L0_ffn_b1"].reshape(E * EH, P).T, "rank": np.arange(E, 0, -1).astype(np.float32),
    }
    arrays = {k: np.ascontiguousarray(v) for k, v in arrays.items()}
    nc = _bacc.Bacc("TRN2", target_bir_lowering=False, num_devices=1)
    io = {k: nc.dram_tensor(k + "_dram", v.shape, mybir.dt.from_np(v.dtype), kind="ExternalInput").ap() for k, v in arrays.items()}
    io["out"] = nc.dram_tensor("out_dram", x.shape, F32, kind="ExternalOutput").ap()
    io["xs"] = nc.dram_tensor("residual_stream", ((L + 1) * NB, P, T // P * D), F32, kind="Internal").ap()
    io["mod"] = nc.dram_tensor("modulation", (NB, 6 * D), F32, kind="Internal").ap()
    for i in range(2):
        io[f"scr{i}"] = nc.dram_tensor(f"parts_dram{i}", (2, 3, P, T), BF16, kind="Internal").ap()
    modulation_program(nc, NB, T, io)
    transformer_program(nc, NB, L, T, io)
    experts_program(nc, NB, L, T, io)
    r = _run(nc, [{k + "_dram": v for k, v in arrays.items()}], core_ids=[0])
    return r.results[0]["out_dram"]
```
